# Optimizing a Trainium2 kernel written in Bass

```python
import numpy as np
import jax
import jax.numpy as jnp

def _softmax(x, axis=-1):
    return jax.nn.softmax(x, axis=axis)

def _gelu(x):
    return jax.nn.gelu(x, approximate=True)

def _silu(x):
    return jax.nn.silu(x)

def _sigmoid(x):
    return jax.nn.sigmoid(x)

def _layernorm(x, axis=-1, eps=1e-05):
    m = jnp.mean(x, axis=axis, keepdims=True)
    v = jnp.var(x, axis=axis, keepdims=True)
    return (x - m) / jnp.sqrt(v + eps)

def _scatter_add(tgt, idx, src, axis=0):
    return tgt.at[idx].add(src)

def _segment_sum(src, seg, n):
    return jax.ops.segment_sum(src, seg, n)
kernel_name = 'mk_seq_preln_d2_jaxref_r8_d6b3ec'

def setup_inputs(seed: int=0):
    np.random.seed(seed)
    _w = jnp.asarray

    def _L0_attn_setup():
        import jax, jax.numpy as jnp
        import numpy as np
        B, S, E, H, Dh = (2, 256, 128, 16, 64)
        key = jax.random.key(seed)
        ks = jax.random.split(key, 8)
        w = 0.02
        return {'x': jax.random.normal(ks[0], (B, S, E), jnp.float32), 'Wq': jax.random.normal(ks[1], (H, Dh, E), jnp.float32) * w, 'bq': jax.random.normal(ks[2], (H, Dh), jnp.float32) * w, 'Wk': jax.random.normal(ks[3], (H, Dh, E), jnp.float32) * w, 'bk': jax.random.normal(ks[4], (H, Dh), jnp.float32) * w, 'Wv': jax.random.normal(ks[5], (H, Dh, E), jnp.float32) * w, 'bv': jax.random.normal(ks[6], (H, Dh), jnp.float32) * w, 'proj': jax.random.normal(ks[7], (H * Dh, E), jnp.float32) * w}
    _L0_attn_in = _L0_attn_setup()

    def _L0_ffn_setup():
        import jax, jax.numpy as jnp
        import numpy as np
        B, C, D, O = (4, 512, 128, 128)
        PROJ = 32
        RANKS = [1, 2, 4, 8]
        E = len(RANKS)
        CLAMP_MAX = float(np.log(1.0 / 0.01))

        def _l2norm(v, axis):
            return v / jnp.maximum(jnp.linalg.norm(v, axis=axis, keepdims=True), 1e-12)
        key = jax.random.key(seed)
        ks = jax.random.split(key, 16)
        inp = {'x': jax.random.normal(ks[0], (B, C, D), dtype=jnp.float32), 'W': jax.random.normal(ks[1], (O, D), dtype=jnp.float32) / np.sqrt(D), 'Wp': jax.random.normal(ks[2], (PROJ, D), dtype=jnp.float32) / np.sqrt(D), 'bp': jnp.zeros((PROJ,), dtype=jnp.float32), 'sim': jax.random.normal(ks[3], (PROJ, E), dtype=jnp.float32) * 0.01, 'temp': jnp.full((1,), np.log(1.0 / 0.5), dtype=jnp.float32)}
        for i, r in enumerate(RANKS):
            inp[f'Wd{i}'] = jax.random.normal(ks[4 + 2 * i], (r, D), dtype=jnp.float32) / r
            inp[f'Wu{i}'] = jax.random.normal(ks[5 + 2 * i], (O, r), dtype=jnp.float32) * 0.01
        return inp
    _L0_ffn_in = _L0_ffn_setup()

    def _L1_attn_setup():
        import jax, jax.numpy as jnp
        import numpy as np
        NUM_HEADS = 16
        key = jax.random.key(seed)
        k1, k2, k3, k4 = jax.random.split(key, 4)
        d_model = 128
        B, S = (4, 256)
        scale = 1.0 / np.sqrt(d_model)
        x = jax.random.normal(k1, (B, S, d_model), dtype=jnp.float32)
        W_k = jax.random.normal(k2, (d_model, d_model), dtype=jnp.float32) * scale
        W_v = jax.random.normal(k3, (d_model, d_model), dtype=jnp.float32) * scale
        W_o = jax.random.normal(k4, (d_model, d_model), dtype=jnp.float32) * scale
        return {'x': x, 'W_k': W_k, 'W_v': W_v, 'W_o': W_o}
    _L1_attn_in = _L1_attn_setup()

    def _L1_ffn_setup():
        import jax, jax.numpy as jnp
        import numpy as np
        B, T, C = (2, 64, 128)
        I = 512
        E = 8
        K = 2
        key = jax.random.key(seed)
        ks = jax.random.split(key, 8)
        s = 0.02
        return {'x': jax.random.normal(ks[0], (B, T, C), jnp.float32), 'Wr1': jax.random.normal(ks[1], (C, C // 4), jnp.float32) * s, 'br1': jnp.zeros((C // 4,), jnp.float32), 'Wr2': jax.random.normal(ks[2], (C // 4, E), jnp.float32) * s, 'br2': jnp.zeros((E,), jnp.float32), 'Ws1': jax.random.normal(ks[3], (C, I), jnp.float32) * s, 'bs1': jnp.zeros((I,), jnp.float32), 'Ws2': jax.random.normal(ks[4], (I, C), jnp.float32) * s, 'bs2': jnp.zeros((C,), jnp.float32), 'We1': jax.random.normal(ks[5], (E, C, I), jnp.float32) * s, 'be1': jnp.zeros((E, I), jnp.float32), 'We2': jax.random.normal(ks[6], (E, I, C), jnp.float32) * s, 'be2': jnp.zeros((E, C), jnp.float32)}
    _L1_ffn_in = _L1_ffn_setup()
    _d = {'L0_attn_x': _L0_attn_in['x'], 'L0_attn_Wq': _L0_attn_in['Wq'], 'L0_attn_bq': _L0_attn_in['bq'], 'L0_attn_Wk': _L0_attn_in['Wk'], 'L0_attn_bk': _L0_attn_in['bk'], 'L0_attn_Wv': _L0_attn_in['Wv'], 'L0_attn_bv': _L0_attn_in['bv'], 'L0_attn_proj': _L0_attn_in['proj'], 'L0_ffn_W': _L0_ffn_in['W'], 'L0_ffn_Wp': _L0_ffn_in['Wp'], 'L0_ffn_bp': _L0_ffn_in['bp'], 'L0_ffn_sim': _L0_ffn_in['sim'], 'L0_ffn_temp': _L0_ffn_in['temp'], 'L0_ffn_Wd0': _L0_ffn_in['Wd0'], 'L0_ffn_Wu0': _L0_ffn_in['Wu0'], 'L0_ffn_Wd1': _L0_ffn_in['Wd1'], 'L0_ffn_Wu1': _L0_ffn_in['Wu1'], 'L0_ffn_Wd2': _L0_ffn_in['Wd2'], 'L0_ffn_Wu2': _L0_ffn_in['Wu2'], 'L0_ffn_Wd3': _L0_ffn_in['Wd3'], 'L0_ffn_Wu3': _L0_ffn_in['Wu3'], 'L1_attn_W_k': _L1_attn_in['W_k'], 'L1_attn_W_v': _L1_attn_in['W_v'], 'L1_attn_W_o': _L1_attn_in['W_o'], 'L1_ffn_Wr1': _L1_ffn_in['Wr1'], 'L1_ffn_br1': _L1_ffn_in['br1'], 'L1_ffn_Wr2': _L1_ffn_in['Wr2'], 'L1_ffn_br2': _L1_ffn_in['br2'], 'L1_ffn_Ws1': _L1_ffn_in['Ws1'], 'L1_ffn_bs1': _L1_ffn_in['bs1'], 'L1_ffn_Ws2': _L1_ffn_in['Ws2'], 'L1_ffn_bs2': _L1_ffn_in['bs2'], 'L1_ffn_We1': _L1_ffn_in['We1'], 'L1_ffn_be1': _L1_ffn_in['be1'], 'L1_ffn_We2': _L1_ffn_in['We2'], 'L1_ffn_be2': _L1_ffn_in['be2']}
    _x0 = _d['L0_attn_x']
    _d['L0_attn_x'] = jax.random.normal(jax.random.fold_in(jax.random.key(seed), 1), (2, 1024, 128), dtype=_x0.dtype)
    del _x0
    return _d

def reference(L0_attn_x, L0_attn_Wq, L0_attn_bq, L0_attn_Wk, L0_attn_bk, L0_attn_Wv, L0_attn_bv, L0_attn_proj, L0_ffn_W, L0_ffn_Wp, L0_ffn_bp, L0_ffn_sim, L0_ffn_temp, L0_ffn_Wd0, L0_ffn_Wu0, L0_ffn_Wd1, L0_ffn_Wu1, L0_ffn_Wd2, L0_ffn_Wu2, L0_ffn_Wd3, L0_ffn_Wu3, L1_attn_W_k, L1_attn_W_v, L1_attn_W_o, L1_ffn_Wr1, L1_ffn_br1, L1_ffn_Wr2, L1_ffn_br2, L1_ffn_Ws1, L1_ffn_bs1, L1_ffn_Ws2, L1_ffn_bs2, L1_ffn_We1, L1_ffn_be1, L1_ffn_We2, L1_ffn_be2):

    def _L0_attn_ref(x, Wq, bq, Wk, bk, Wv, bv, proj):
        import jax, jax.numpy as jnp
        import numpy as np
        B, S, E, H, Dh = (2, 256, 128, 16, 64)
        b, s, e = x.shape
        h, dh, _ = Wq.shape
        scale = jnp.sqrt(jnp.asarray(dh, x.dtype))
        q = jnp.einsum('bse,hde->bhsd', x, Wq) + bq[None, :, None, :]
        k = jnp.einsum('bse,hde->bhsd', x, Wk) + bk[None, :, None, :]
        v = jnp.einsum('bse,hde->bhsd', x, Wv) + bv[None, :, None, :]
        causal = jnp.triu(jnp.ones((s, s), bool), 1)
        scores = jnp.einsum('bhsd,bhtd->bhst', q, k) / scale
        scores = jnp.where(causal[None, None], -jnp.inf, scores)
        att = jax.nn.softmax(scores, axis=-1) / scale
        z = jnp.einsum('bhst,bhtd->bhsd', att, v)
        z = z.reshape(b, s, h * dh)
        return z @ proj

    def _L0_ffn_ref(x, W, Wp, bp, sim, temp, Wd0, Wu0, Wd1, Wu1, Wd2, Wu2, Wd3, Wu3):
        import jax, jax.numpy as jnp
        import numpy as np
        B, C, D, O = (4, 512, 128, 128)
        PROJ = 32
        RANKS = [1, 2, 4, 8]
        E = len(RANKS)
        CLAMP_MAX = float(np.log(1.0 / 0.01))

        def _l2norm(v, axis):
            return v / jnp.maximum(jnp.linalg.norm(v, axis=axis, keepdims=True), 1e-12)
        base = jnp.einsum('bcd,od->bco', x, W)
        xf = x.reshape(-1, x.shape[-1])
        proj = _l2norm(xf @ Wp.T + bp, axis=1)
        simn = _l2norm(sim, axis=0)
        scale = jnp.exp(jnp.minimum(temp, CLAMP_MAX))
        logits = proj @ simn * scale
        lw = jax.nn.softmax(logits, axis=1)
        top1 = jnp.argmax(lw, axis=1)
        ret = jnp.where(jnp.arange(E)[None, :] == top1[:, None], lw, 0.0)
        ret = ret.reshape(x.shape[0], x.shape[1], E)
        downs = (Wd0, Wd1, Wd2, Wd3)
        ups = (Wu0, Wu1, Wu2, Wu3)
        l = jnp.stack([jnp.einsum('bcr,or->bco', jnp.einsum('bcd,rd->bcr', x, d), u) for d, u in zip(downs, ups)], axis=2)
        res = jnp.sum(ret[..., None] * l, axis=2)
        return base + res

    def _L1_attn_ref(x, W_k, W_v, W_o):
        import jax, jax.numpy as jnp
        import numpy as np
        NUM_HEADS = 16
        B, S, D = x.shape
        H = NUM_HEADS
        dk = D // H
        inv_sqrt_dk = 1.0 / jnp.sqrt(jnp.asarray(dk, dtype=x.dtype))
        Q = (x @ W_k.T).reshape(B, S, H, dk).transpose(0, 2, 1, 3)
        sq_norm = jnp.sum(Q * Q, axis=-1, keepdims=True)
        dot = jnp.einsum('bhsk,bhtk->bhst', Q, Q)
        squared_dist = sq_norm - 2.0 * dot + sq_norm.transpose(0, 1, 3, 2)
        scores = -squared_dist * inv_sqrt_dk
        attn = jax.nn.softmax(scores, axis=-1)
        context_q = jnp.einsum('bhst,bhtk->bhsk', attn, Q)
        Wq_h = W_k.reshape(H, dk, D)
        Wv_h = W_v.reshape(H, dk, D)
        merged = jnp.einsum('hkd,hvd->hkv', Wq_h, Wv_h)
        attn_out = jnp.einsum('bhsk,hkv->bhsv', context_q, merged) * inv_sqrt_dk
        attn_out = attn_out.transpose(0, 2, 1, 3).reshape(B, S, D)
        return attn_out @ W_o.T

    def _L1_ffn_ref(x, Wr1, br1, Wr2, br2, Ws1, bs1, Ws2, bs2, We1, be1, We2, be2):
        import jax, jax.numpy as jnp
        import numpy as np
        B, T, C = (2, 64, 128)
        I = 512
        E = 8
        K = 2
        Bb, Tt, Cc = x.shape
        xf = x.reshape(-1, Cc)
        logits = jax.nn.relu(xf @ Wr1 + br1) @ Wr2 + br2
        gates = jax.nn.softmax(logits, axis=-1)
        tg, ti = jax.lax.top_k(gates, K)
        tg = jax.nn.softmax(tg / K, axis=-1)
        out = jax.nn.silu(xf @ Ws1 + bs1) @ Ws2 + bs2
        for e in range(E):
            h = jax.nn.silu(xf @ We1[e] + be1[e]) @ We2[e] + be2[e]
            w = jnp.sum(tg * (ti == e), axis=-1)
            out = out + w[:, None] * h
        return out.reshape(Bb, Tt, Cc)
    x = L0_attn_x
    x = x + _L0_attn_ref(_layernorm(x, axis=-1), L0_attn_Wq, L0_attn_bq, L0_attn_Wk, L0_attn_bk, L0_attn_Wv, L0_attn_bv, L0_attn_proj)
    x = x + _L0_ffn_ref(_layernorm(x, axis=-1), L0_ffn_W, L0_ffn_Wp, L0_ffn_bp, L0_ffn_sim, L0_ffn_temp, L0_ffn_Wd0, L0_ffn_Wu0, L0_ffn_Wd1, L0_ffn_Wu1, L0_ffn_Wd2, L0_ffn_Wu2, L0_ffn_Wd3, L0_ffn_Wu3)
    x = x + _L1_attn_ref(_layernorm(x, axis=-1), L1_attn_W_k, L1_attn_W_v, L1_attn_W_o)
    x = x + _L1_ffn_ref(_layernorm(x, axis=-1), L1_ffn_Wr1, L1_ffn_br1, L1_ffn_Wr2, L1_ffn_br2, L1_ffn_Ws1, L1_ffn_bs1, L1_ffn_Ws2, L1_ffn_bs2, L1_ffn_We1, L1_ffn_be1, L1_ffn_We2, L1_ffn_be2)
    return x

_drawn_inputs = setup_inputs


def setup_inputs(seed=0):
    import zlib

    import numpy as np

    out = dict(_drawn_inputs(seed))
    spreads = {'L0_ffn_bp': (0.0, 0.8),
     'L1_ffn_br1': (0.0, 0.437),
     'L1_ffn_br2': (0.0, 0.1),
     'L1_ffn_bs1': (0.0, 0.577),
     'L1_ffn_bs2': (0.0, 0.1),
     'L1_ffn_be1': (0.0, 0.745),
     'L1_ffn_be2': (0.0, 0.1)}
    factors = {'L0_attn_Wq': 8.0,
     'L0_attn_bq': 8.0,
     'L0_attn_Wk': 8.0,
     'L0_attn_bk': 64.0,
     'L0_attn_Wv': 8.0,
     'L0_attn_bv': 8.0,
     'L0_attn_proj': 8.0,
     'L0_ffn_Wp': 3.074,
     'L0_ffn_sim': 2.953,
     'L0_ffn_Wd0': 3.693,
     'L0_ffn_Wu0': 3.311,
     'L0_ffn_Wd1': 5.465,
     'L0_ffn_Wu1': 5.701,
     'L0_ffn_Wd2': 7.928,
     'L0_ffn_Wu2': 7.901,
     'L0_ffn_Wd3': 8.0,
     'L0_ffn_Wu3': 8.0,
     'L1_ffn_Wr1': 2.755}
    for name, (base, spread) in spreads.items():
        noise = np.random.default_rng([zlib.crc32(name.encode()), seed]).standard_normal(out[name].shape)
        drawn = base * np.exp(spread * noise) if base else spread * noise
        out[name] = jnp.asarray(drawn.astype(out[name].dtype))
    for name, factor in factors.items():
        out[name] = (out[name] * factor).astype(out[name].dtype)
    return out
```

```python
import math
from contextlib import ExitStack

import numpy as np

import concourse.bass as bass
from concourse import mybir

F32, F32R, BF16 = mybir.dt.float32, mybir.dt.float32r, mybir.dt.bfloat16
ACT, ALU, AX = mybir.ActivationFunctionType, mybir.AluOpType, mybir.AxisListType

P = 128
BATCH, SEQ, D = 2, 1024, 128
TOK = BATCH * SEQ
NT, TB = TOK // P, SEQ // P
BLK = 512
EPS = 1e-5

HEADS, DH = 16, 64
PAIRS = HEADS // 2
SCALE0 = 1.0 / math.sqrt(DH)
MROWS = 2 * TB
KB_ROWS = DH + MROWS
UNITS = [(0, t) for t in range(TB // 2)] + [(1, t) for t in range(TB)]
NU = 2 * len(UNITS)
SB0_UNITS = TB
PIECES = [(s, c, min(BLK, P * (s + 1) - c)) for s in range(TB) for c in range(0, P * (s + 1), BLK)]
NPIECE = 2 * len(PIECES)
NP0 = 6
NEG = -1e30

PROJ, RANKS = 32, (1, 2, 4, 8)
NE0, RSUM = len(RANKS), sum(RANKS)
DOWN = PROJ + RSUM + 1
CLAMP = float(np.log(1.0 / 0.01))

DK = 8
GH = 4
GROUPS = HEADS // GH
SCALE1 = 1.0 / math.sqrt(DK)
NSLOT = GH * TB
NP1 = 8

INNER, NE1 = 512, 8
NI = INNER // P
RH = D // 4

C_ID, C_MS, C_MT, C_SEL, C_BD, C_BLK, C_COL = 0, 128, 256, 384, 512, 640, 672
C_MASK = C_COL + 6
C_FIRST = C_MASK + GH
CONSTS = C_FIRST + NE1


def constants():
    c = np.zeros((P, CONSTS), np.float32)
    i = np.arange(P)
    c[:, C_ID:C_ID + P] = np.eye(P)
    c[:, C_MS:C_MS + P] = np.where(i[None, :] > i[:, None], NEG, 0)
    c[:, C_MT:C_MT + P] = np.where(i[None, :] < i[:, None], NEG, 0)
    c[:, C_SEL:C_SEL + P] = i[:, None] == i[None, :] // 32 * 32 + DK
    c[:, C_BD:C_BD + P] = i[:, None] // DK == i[None, :] // DK
    c[:32, C_BLK:C_BLK + 32] = -0.5 * (i[:32, None] // DK == i[None, :32] // DK)
    quad, j = i // 32, i % DK
    hi, lo, one = (0, 1, 0), (1, -1, 0), (0, 0, 1)
    for p in range(P):
        r = [hi, lo, hi][quad[p]] if quad[p] < 3 else {0: hi, 1: lo, 2: one, 3: one}.get(j[p], (0, 0, 0))
        l = [hi, hi, lo][quad[p]] if quad[p] < 3 else {0: one, 1: one, 2: hi, 3: lo}.get(j[p], (0, 0, 0))
        c[p, C_COL:C_COL + 3], c[p, C_COL + 3:C_COL + 6] = r, l
        c[p, C_MASK + p % 32 // DK] = 1
    c[:, C_FIRST:C_FIRST + NE1] = np.arange(NE1, 0, -1)
    m = np.zeros((MROWS, 2, TB, P), np.float32)
    for h in range(2):
        for s in range(TB):
            m[h * TB + s, h, s] = 1
    return c, m.reshape(MROWS, 2 * SEQ)


def build_kernel(nc, a, out, stop):
    ctx = ExitStack()
    with ctx:
        def sb(name, shape, dt=F32):
            return ctx.enter_context(nc.sbuf_tensor(name, shape, dt))

        def sem(name):
            return ctx.enter_context(nc.semaphore(name))

        x = sb("x", [P, NT, D])
        xn = sb("xn", [P, NT, D])
        xT = sb("xT", [P, TOK])
        cst = sb("cst", [P, CONSTS])
        mD = sb("mD", [MROWS, 2, TB, P])
        idb = sb("idb", [P, P], BF16)
        msb = sb("msb", [P, P], BF16)
        mtb = sb("mtb", [P, P], BF16)
        ones = sb("ones", [P, DH])
        st = sb("st", [P, NT, 6])
        mv = sb("mv", [P, NT, 2])
        rs = sb("rs", [P, 4, NT])

        qa = sb("qa", [P, BATCH, 2, SEQ], F32R)
        qb = sb("qb", [P, BATCH, 2, SEQ], F32R)
        ka = sb("ka", [P, BATCH, 2, SEQ], F32R)
        kb = sb("kb", [P, BATCH, 2, SEQ], F32R)
        v = sb("v", [P, BATCH, TB, D])
        wqkv = sb("wqkv", [P, 4 * D + 2])
        wpr = sb("wpr", [P, TB, D])
        pr = sb("pr", [P, NP1, SEQ])
        pacc = sb("pacc", [P, 2, 2, BLK])
        zero = sb("zero", [P, BLK])
        mx = sb("mx", [P, 2, TB])
        mx2 = sb("mx2", [P, 2, TB // 2])
        zsum = sb("zsum", [P, BLK])
        zz = sb("zz", [P, 2, SEQ // 2])

        wdn = sb("wdn", [P, DOWN])
        wbase = sb("wbase", [P, D])
        wup = sb("wup", [RSUM + 1, D])
        small = sb("small", [P, PROJ + NE0 * PROJ + 1])
        dn = sb("dn", [P, NT, DOWN])
        pj = sb("pj", [P, NT, PROJ])
        sq = sb("sq", [P, NT, PROJ])
        prod = xn[:, :, :].rearrange("p n (e k) -> p n e k", e=NE0)
        simq = sb("simq", [P, NE0, PROJ])
        nrm = sb("nrm", [P, NT + NE0])
        escale = sb("escale", [P, 1])
        lg = sb("lg", [P, NT, NE0])
        lw = sb("lw", [P, NT, NE0])
        col = sb("col", [P, 4, NT])
        hg = sb("hg", [P, NT, RSUM + 1])
        hgT = mD[:, :, :, :].rearrange("r h s c -> r (h s c)")

        r1 = qa[:, :, 0, :]
        hi1 = qa[:, :, 1, :]
        l1 = qb[:, :, 0, :]

        def l1h(b, h):
            return (ka, kb)[h // 2][:, b, h % 2, :]
        wk3 = sb("wk3", [P, 3 * GH * DK])
        wkT = sb("wkT", [P, D])
        wvT = sb("wvT", [P, D])
        woT = sb("woT", [P, D])
        a1 = sb("a1", [P, GROUPS, GH, 32])
        gg = sb("gg", [P, GROUPS, D])
        qtm = xn
        qv = v[:, :, :, :].rearrange("p b t (h j) -> p b t h j", j=32)
        sq1 = sb("sq1", [3 * GH * DK, SEQ])
        zs = pacc[:, 0, :, :].rearrange("p h c -> p (h c)")
        rz = pacc[:, 1, :, :].rearrange("p h c -> p (h c)")
        zn = zz[:, :, :].rearrange("p h c -> p (h c)")

        w1 = sb("w1", [P, 2, 2 * INNER + NI])
        b2 = sb("b2", [1 + NE1, D])
        wr = sb("wr", [P, RH + 1])
        wr2 = sb("wr2", [RH + 1, NE1])
        rT = pacc[0:RH + 1, :, :, :].rearrange("p k h c -> p (k h c)")
        gl = sb("gl", [P, NT, NE1])
        ga = sb("ga", [P, NT, NE1])
        oh1 = sb("oh1", [P, NT, NE1])
        oh2 = sb("oh2", [P, NT, NE1])
        gw = sb("gw", [P, NT, 1 + NE1])
        gwT = v[0:1 + NE1, :, :, :].rearrange("p b t d -> p (b t d)")
        hid = pr[:, 0:4, :].rearrange("p (b i) (k c) -> p b (i k) c", b=2, k=2)

        banks = ctx.enter_context(nc.psum_tensor("banks", [P, 8, BLK], F32))

        ident = cst[:, C_ID:C_ID + P]
        block = ctx.enter_context(nc.Block())

        s_x = [sem(f"x_in{i}") for i in range(4)]
        s_const, s_maskd = sem("const_in"), sem("maskd_in")
        s_wq, s_wp = sem("wqkv_in"), sem("wproj_in")
        s_out = sem("out_done")
        s_setup = sem("setup_done")
        N_SETUP = 7
        ln = [{n: sem(f"ln{k}_{n}") for n in ("stats", "aggr", "ln", "rstd", "newton", "norm", "turned", "xT")} for k in range(4)]
        s_prep_qk, s_prep_v, s_prep_m, s_prep_t = sem("qk_projected"), sem("v_projected"), sem("piece_scored"), sem("max_turned")
        s_qk_hi, s_qk_lo, s_v = sem("qk_hi_done"), sem("qk_lo_done"), sem("v_stored")
        s_pmax, s_mneg, s_mrow = sem("piece_max"), sem("max_negated"), sem("max_rows")
        s_st, s_exp, s_padd, s_pv = sem("scored"), sem("exp_done"), sem("prob_added"), sem("pv_done")
        s_sum, s_zsum, s_zz, s_op, s_xacc = sem("sums_done"), sem("sums_inverted"), sem("z_ready"), sem("out_projected"), sem("x_added")

        s_fw = sem("linear_weights_in")
        s_dn, s_dne, s_ch, s_fa, s_hT, s_hTe, s_fo, s_fx = (sem(n) for n in (
            "down_projected", "down_stored", "router_chain", "router_act", "gated_turned", "gated_stored", "linear_done", "linear_added"))
        s_aw, s_wk = sem("attn1_weights_in"), sem("wk3_in")
        s_a1, s_a1m, s_gg, s_gge, s_qt, s_qte = (sem(n) for n in (
            "merged_done", "merged_masked", "merged_wo_done", "merged_wo_stored", "qtm_done", "qtm_stored"))
        s_pj, s_sq, s_nm, s_hi, s_rl, s_lh, s_qv = (sem(n) for n in (
            "q_projected", "q_squared", "norms_done", "q_rounded", "sides_filled", "heads_masked", "qv_filled"))
        s_st1, s_exp1, s_pv1, s_zs, s_sum1, s_rz, s_zn, s_op1, s_x1 = (sem(n) for n in (
            "dist_scored", "dist_exp", "dist_pv", "ctx_stored", "ctx_sums", "ctx_recip", "ctx_ready", "ctx_projected", "attn1_added"))
        s_mw, s_ew = sem("moe_weights_in"), [sem("expert_in0"), sem("expert_in1")]
        s_rh, s_rhe, s_lo, s_gc, s_ga, s_gT, s_gTe, s_b2, s_up, s_hid, s_down, s_xe = (sem(n) for n in (
            "router_hidden", "router_relu", "router_logits", "gate_chain", "gate_act", "gates_turned", "gates_stored", "bias_done",
            "up_done", "silu_done", "down_done", "expert_added"))

        def ln_dve(v_, k, ready):
            s = ln[k]
            for n in range(NT):
                ready(v_, n)
                v_.bn_stats(out=st[:, n, :], in_=x[:, n, :]).then_inc(s["stats"], 1)
            v_.wait_ge(s["stats"], NT)
            for n in range(NT):
                v_.bn_aggr(out=mv[:, n, :], in_=st[:, n, :]).then_inc(s["aggr"], 1)
            v_.wait_ge(s["aggr"], NT)
            v_.tensor_scalar(rs[:, 0, :], mv[:, :, 1], EPS, None, ALU.add).then_inc(s["aggr"], 1)
            v_.wait_ge(s["rstd"], 1)
            v_.tensor_tensor(rs[:, 3, :], rs[:, 2, :], rs[:, 2, :], ALU.mult).then_inc(s["newton"], 1)
            v_.wait_ge(s["newton"], 1)
            v_.tensor_tensor(rs[:, 3, :], rs[:, 3, :], rs[:, 0, :], ALU.mult).then_inc(s["newton"], 1)
            v_.wait_ge(s["newton"], 2)
            v_.tensor_scalar(rs[:, 3, :], rs[:, 3, :], -0.5, 1.5, ALU.mult, ALU.add).then_inc(s["newton"], 1)
            v_.wait_ge(s["newton"], 3)
            v_.tensor_tensor(rs[:, 3, :], rs[:, 3, :], rs[:, 2, :], ALU.mult).then_inc(s["newton"], 1)
            v_.wait_ge(s["newton"], 4)
            for n in range(NT):
                v_.tensor_scalar(xn[:, n, :], x[:, n, :], mv[:, n, 0:1], rs[:, 3, n:n + 1],
                                 ALU.subtract, ALU.mult).then_inc(s["norm"], 1)

        def ln_act(act, k):
            s = ln[k]
            act.wait_ge(s["aggr"], NT + 1)
            act.activation(rs[:, 1, :], rs[:, 0, :], ACT.Ln).then_inc(s["ln"], 1)
            act.wait_ge(s["ln"], 1)
            act.activation(rs[:, 2, :], rs[:, 1, :], ACT.Exp, scale=-0.5).then_inc(s["rstd"], 1)
            for i in range(4):
                act.wait_ge(s["turned"], i + 1)
                act.activation(xT[:, i * BLK:(i + 1) * BLK], banks[:, i, :], ACT.Copy).then_inc(s["xT"], 1)

        def ln_pe(pe, k):
            s = ln[k]
            for i in range(4):
                pe.wait_ge(s["norm"], 4 * i + 4)
                for j in range(4):
                    mm = pe.transpose(banks[:, i, j * P:(j + 1) * P], xn[:, 4 * i + j, :], ident)
                mm.then_inc(s["turned"], 1)

        I_T = 4 + NPIECE
        I_V = I_T + 1
        NITEM = I_V + 2
        PREP_AT = {0: [0], 1: [1], 2: [2], 3: [3]}
        for n in range(NPIECE):
            PREP_AT.setdefault(5 + n // 2, []).append(4 + n)
        PREP_AT.setdefault(19, []).append(I_T)
        PREP_AT.setdefault(21, []).append(I_V)
        PREP_AT.setdefault(22, []).append(I_V + 1)
        TAIL0_SUM = 11
        TAIL1_SUM, TAIL1_OUT = 2, 4

        def pbank(n):
            return banks[:, (3, 7)[n % 2], :]

        def released(n):
            if n < 4:
                return s_qk_lo, 4, n
            if n < I_T:
                return s_pmax, NPIECE, n - 4
            if n == I_T:
                return s_mrow, 2, 1
            return s_v, 2, n - I_V

        def wait_item(e, u, n):
            s, per, k = released(n)
            e.wait_ge(s, u * per + k + 1)

        def piece(n):
            return (n // len(PIECES),) + PIECES[n % len(PIECES)]

        def unit(j):
            sbk, t = UNITS[j // 2]
            return j % 2, sbk, t, max(0, P * t - BLK * sbk)

        def pe_item(pe, u, b, n, first):
            if n >= 2:
                wait_item(pe, u, n - 2)
            elif not first:
                wait_item(pe, u - 1, NITEM - 1 if n == 0 else NITEM - 2)
            dst = pbank(n)
            if n < 4:
                if n == 0 and b == 0:
                    pe.wait_ge(s_wq, 8 * u + 16)
                w = wqkv[:, (n // 2) * D:(n // 2 + 1) * D]
                c = b * SEQ + (n % 2) * BLK
                pe.matmul(dst, w, xT[:, c:c + BLK], start=True, stop=True).then_inc(s_prep_qk, 1)
            elif n < I_T:
                h, s, c, w = piece(n - 4)
                if n == 4:
                    pe.wait_ge(s_qk_lo, u * 4 + 4)
                diag = c + w == P * (s + 1)
                mm = pe.matmul(dst[:, 0:w], qa[:, b, h, s * P:(s + 1) * P], ka[:, b, h, c:c + w], start=True, stop=not diag)
                if diag:
                    mm = pe.matmul(dst[:, w - P:w], idb[:, :], msb[:, :], start=False, stop=True)
                mm.then_inc(s_prep_m, 1)
            elif n == I_T:
                pe.wait_ge(s_mneg, 2 * u + 2)
                pe.transpose(dst[0:MROWS, 0:P], mx[:, :, :].rearrange("p h s -> p (h s)"), ident).then_inc(s_prep_t, 1)
            else:
                half = n - I_V
                for t in range(4):
                    c = b * SEQ + (4 * half + t) * P
                    mm = pe.matmul(dst[:, t * P:(t + 1) * P], xT[:, c:c + P], wqkv[:, 2 * D:3 * D], start=True, stop=True)
                mm.then_inc(s_prep_v, 1)

        def act_item(act, u, b, n):
            src = pbank(n)
            if n < 4:
                c = slice((n % 2) * BLK, (n % 2 + 1) * BLK)
                act.wait_ge(s_prep_qk, 4 * u + n + 1)
                bias = wqkv[:, 4 * D + n // 2:4 * D + n // 2 + 1]
                if n < 2:
                    for h in range(2):
                        for r in range(2):
                            i = act.activation(qa[r * DH:(r + 1) * DH, b, h, c], src[h * DH:(h + 1) * DH, :], ACT.Identity,
                                               bias=bias[h * DH:(h + 1) * DH, :])
                else:
                    for h in range(2):
                        for dst in (ka, kb) if h == 0 else (ka, kb, None):
                            o = ka[DH:P, b, h, c] if dst is None else dst[0:DH, b, h, c]
                            i = act.activation(o, src[h * DH:(h + 1) * DH, :], ACT.Identity,
                                               bias=bias[h * DH:(h + 1) * DH, :])
                i.then_inc(s_qk_hi, 1)

        def dve_item(dve, u, b, n, first):
            src = pbank(n)
            if n < 4:
                c = slice((n % 2) * BLK, (n % 2 + 1) * BLK)
                bias = wqkv[:, 4 * D + n // 2:4 * D + n // 2 + 1]
                dve.wait_ge(s_qk_hi, 4 * u + n + 1)
                for h in range(2):
                    hp = slice(h * DH, (h + 1) * DH)
                    if n < 2:
                        o, hi = qb[0:DH, b, h, c], qa[hp, b, h, c]
                    else:
                        o, hi = ka[DH:P, b, h, c], ka[hp, b, h, c]
                    i = dve.scalar_tensor_tensor(out=o, in0=src[hp, :], scalar=bias[hp, :], in1=hi, op0=ALU.add, op1=ALU.subtract)
                i.then_inc(s_qk_lo, 1)
            elif n < I_T:
                h, s, c, w = piece(n - 4)
                dve.wait_ge(s_prep_m, NPIECE * u + n - 4 + 1)
                if n == 4 and not first:
                    dve.wait_ge(s_prep_t, u)
                o = mx[:, h, s:s + 1] if c == 0 else mx2[:, h, s - TB // 2:s - TB // 2 + 1]
                dve.tensor_reduce(o, src[:, 0:w], AX.X, ALU.max).then_inc(s_pmax, 1)
                if n == I_T - 1:
                    dve.wait_ge(s_pmax, NPIECE * (u + 1))
                    dve.tensor_tensor(mx[:, :, TB // 2:TB], mx[:, :, TB // 2:TB], mx2[:, :, :], ALU.max).then_inc(s_mneg, 1)
                    dve.wait_ge(s_mneg, 2 * u + 1)
                    dve.tensor_scalar(mx[:, :, :], mx[:, :, :], -1.0, None, ALU.mult).then_inc(s_mneg, 1)
            elif n == I_T:
                dve.wait_ge(s_prep_t, u + 1)
                for h in range(2):
                    o = qb[DH:KB_ROWS, b, h, :].rearrange("r (s c) -> r s c", s=TB)
                    src3 = src[0:MROWS, 0:P].rearrange("r (o c) -> r o c", o=1).to_broadcast([MROWS, TB, P])
                    dve.tensor_tensor(o, src3, mD[:, h, :, :], ALU.mult).then_inc(s_mrow, 1)
            else:
                half = n - I_V
                dve.wait_ge(s_prep_v, 2 * u + half + 1)
                bv = wqkv[:, 3 * D:4 * D].rearrange("p (o d) -> p o d", o=1).to_broadcast([P, 4, D])
                dve.tensor_tensor(v[:, b, 4 * half:4 * half + 4, :], src.rearrange("p (t d) -> p t d", t=4), bv, ALU.add).then_inc(s_v, 1)

        def pe_scores(pe, u, b, j):
            h, sbk, t, o = unit(j)
            w = BLK - o
            if j == 0:
                pe.wait_ge(s_mrow, 2 * u + 2)
                pe.wait_ge(s_v, 2 * u + 2)
            dst = banks[:, j % 3, 0:w]
            q = slice(sbk * BLK + o, (sbk + 1) * BLK)
            k = slice(t * P, (t + 1) * P)
            diag = P * t >= BLK * sbk
            pe.matmul(dst, ka[:, b, h, k], qa[:, b, h, q], start=True, stop=False)
            mm = pe.matmul(dst, kb[0:KB_ROWS, b, h, k], qb[0:KB_ROWS, b, h, q], start=False, stop=not diag)
            if diag:
                mm = pe.matmul(dst[:, 0:P], idb[:, :], mtb[:, :], start=False, stop=True)
            mm.then_inc(s_st, 1)

        def pe_pv(pe, u, b, j, first):
            h, sbk, t, o = unit(j)
            pe.wait_ge(s_exp, NU * u + j + 1)
            if t == 0 and h == 0 and not first:
                pe.wait_ge(s_zz, 2 * u + sbk - 1)
            pe.matmul(banks[h * DH:(h + 1) * DH, 4 + sbk, o:BLK], v[:, b, t, h * DH:(h + 1) * DH],
                      pr[:, j % NP0, 0:BLK - o], start=(t == 0),
                      stop=(t == (sbk + 1) * TB // 2 - 1)).then_inc(s_pv, 1)

        def pe_sums(pe, u, sbk, first):
            pe.wait_ge(s_padd, NU * u + (SB0_UNITS if sbk == 0 else NU))
            if sbk == 1:
                pe.wait_ge(s_zsum, 2 * u + 1)
            elif not first:
                pe.wait_ge(s_xacc, u)
            for h in range(2):
                mm = pe.matmul(banks[h * DH:(h + 1) * DH, 6, :], ones[:, :], pacc[:, sbk, h, :], start=True, stop=True)
            mm.then_inc(s_sum, 1)

        def pe_out(pe, u, b, p):
            pe.wait_ge(s_zz, 2 * u + 2)
            for i in range(TB):
                for h in range(2):
                    mm = pe.matmul(banks[h * DH:(h + 1) * DH, 6, 0:D], zz[:, h, i:SEQ // 2:TB], wpr[:, i, :],
                                   start=(i == 0), stop=(i == TB - 1))
            mm.then_inc(s_op, 1)

        def dve_norm(dve, u, b, sbk, first):
            n = 2 * u + sbk
            dve.wait_ge(s_sum, n + 1)
            if not (first and sbk == 0):
                dve.wait_ge(s_zz, n)
            dve.reciprocal(zsum[:, :], banks[:, 6, :]).then_inc(s_zsum, 1)
            dve.wait_ge(s_zsum, n + 1)
            dve.wait_ge(s_pv, NU * u + (SB0_UNITS if sbk == 0 else NU))
            if sbk == 0 and not first:
                dve.wait_ge(s_op, u)
            half = BLK // 2
            for h in range(2):
                hp = slice(h * DH, (h + 1) * DH)
                for odd in range(2):
                    i = dve.tensor_tensor(zz[odd * DH:(odd + 1) * DH, h, sbk * half:(sbk + 1) * half],
                                          banks[hp, 4 + sbk, odd:BLK:2], zsum[hp, odd:BLK:2], ALU.mult)
            i.then_inc(s_zz, 1)

        def dve_acc(dve, u, b, p):
            dve.wait_ge(s_op, u + 1)
            xs = x[:, b * TB + p, :] if isinstance(p, int) else x[:, bass.ds(b * TB + p, 1), :].rearrange("p o d -> p (o d)")
            dve.scalar_tensor_tensor(out=xs, in0=banks[:, 6, 0:D], scalar=SCALE0, in1=xs, op0=ALU.mult, op1=ALU.add).then_inc(s_xacc, 1)

        def attention0(e, prep, slot, tail_sum, tail_out, rest):
            prep(e, 0, 0, None, True)

            def pair(p, first, last):
                for b in range(BATCH):
                    u = 2 * p + b
                    f, l = first and b == 0, last and b == 1
                    for j in range(NU):
                        slot(e, u, b, j, f)
                        if not l:
                            for n in PREP_AT.get(j, ()):
                                prep(e, u + 1, 1 - b, n, False)
                        if j == TAIL1_SUM and not f:
                            tail_sum(e, u - 1, 1 - b, 1, False)
                        if j == TAIL1_OUT and not f:
                            tail_out(e, u - 1, 1 - b, p - 1 + b)
                        if j == TAIL0_SUM:
                            tail_sum(e, u, b, 0, f)
                        rest(e, u, b, j, f)
            pair(0, True, False)
            with e.Fori(1, PAIRS - 1) as p:
                pair(p, False, False)
            pair(PAIRS - 1, False, True)
            tail_sum(e, 2 * PAIRS - 1, 1, 1, False)
            tail_out(e, 2 * PAIRS - 1, 1, PAIRS - 1)

        def linear_pe(pe):
            pe.wait_ge(s_fw, 64)
            pe.wait_ge(ln[1]["xT"], 4)
            for n in range(NT):
                mm = pe.matmul(banks[:, 4 + n // TB, (n % TB) * DOWN:(n % TB + 1) * DOWN], xT[:, n * P:(n + 1) * P], wdn[:, :],
                               start=True, stop=True)
                if n % TB == TB - 1:
                    mm.then_inc(s_dn, 1)
            pe.wait_ge(s_ch, 24)
            for n in range(NT):
                mm = pe.transpose(banks[0:RSUM + 1, (6, 7, 4, 5)[n // 4], (n % 4) * P:(n % 4 + 1) * P], hg[:, n, :], ident)
                if n % 4 == 3:
                    mm.then_inc(s_hT, 1)
            for n in range(NT):
                if n % 4 == 0:
                    pe.wait_ge(s_hTe, n // 4 + 1)
                o = banks[:, n // 4, (n % 4) * P:(n % 4 + 1) * P]
                pe.matmul(o, xT[:, n * P:(n + 1) * P], wbase[:, :], start=True, stop=False)
                mm = pe.matmul(o, hgT[:, n * P:(n + 1) * P], wup[:, :], start=False, stop=True)
                if n % 4 == 3:
                    mm.then_inc(s_fo, 1)

        def linear_act(act):
            for i in range(2):
                act.wait_ge(s_dn, i + 1)
                act.activation(dn[:, i * TB:(i + 1) * TB, :].rearrange("p n c -> p (n c)"), banks[:, 4 + i, 0:TB * DOWN], ACT.Copy)\
                   .then_inc(s_dne, 1)
            act.wait_ge(s_ch, 5)
            act.activation(nrm[:, :], nrm[:, :], ACT.Sqrt).then_inc(s_fa, 1)
            act.wait_ge(s_ch, 6)
            act.activation(escale[:, :], escale[:, :], ACT.Exp).then_inc(s_fa, 1)
            act.wait_ge(s_ch, 15)
            act.activation(lg[:, :, :], lg[:, :, :], ACT.Exp).then_inc(s_fa, 1)
            for i in range(4):
                act.wait_ge(s_hT, i + 1)
                act.activation(hgT[:, i * BLK:(i + 1) * BLK], banks[0:RSUM + 1, (6, 7, 4, 5)[i], :], ACT.Copy).then_inc(s_hTe, 1)

        def linear_dve(dve):
            done = [0]

            def step(ins, wait=True):
                ins.then_inc(s_ch, 1)
                done[0] += 1
                if wait:
                    dve.wait_ge(s_ch, done[0])

            def wide(t, n):
                return t.rearrange("p (n o) -> p n o", o=1).to_broadcast([P, t.shape[1], n])
            sim = small[:, PROJ:PROJ + NE0 * PROJ].rearrange("p (e k) -> p e k", e=NE0)
            dve.wait_ge(s_fw, 64)
            dve.wait_ge(s_dne, 2)
            step(dve.tensor_tensor(pj[:, :, :], dn[:, :, 0:PROJ],
                                   small[:, 0:PROJ].rearrange("p (o k) -> p o k", o=1).to_broadcast([P, NT, PROJ]), ALU.add))
            step(dve.tensor_tensor(sq[:, :, :], pj[:, :, :], pj[:, :, :], ALU.mult))
            step(dve.tensor_tensor(simq[:, :, :], sim, sim, ALU.mult))
            step(dve.tensor_reduce(nrm[:, 0:NT], sq[:, :, :], AX.X, ALU.add), False)
            step(dve.tensor_reduce(nrm[:, NT:NT + NE0], simq[:, :, :], AX.X, ALU.add), False)
            step(dve.tensor_scalar(escale[:, :], small[:, PROJ + NE0 * PROJ:], CLAMP, None, ALU.min), False)
            dve.wait_ge(ln[1]["turned"], 4)
            step(dve.tensor_tensor(prod, pj[:, :, :].rearrange("p n (o k) -> p n o k", o=1).to_broadcast([P, NT, NE0, PROJ]),
                                   sim.rearrange("p (o e) k -> p o e k", o=1).to_broadcast([P, NT, NE0, PROJ]), ALU.mult))
            step(dve.tensor_reduce(lw[:, :, :], prod, AX.X, ALU.add), False)
            dve.wait_ge(s_fa, 1)
            step(dve.tensor_scalar(nrm[:, :], nrm[:, :], 1e-12, None, ALU.max))
            step(dve.reciprocal(nrm[:, :], nrm[:, :]))
            dve.wait_ge(s_fa, 2)
            step(dve.tensor_scalar(nrm[:, NT:], nrm[:, NT:], escale[:, 0:1], None, ALU.mult))
            step(dve.tensor_tensor(lw[:, :, :], lw[:, :, :], wide(nrm[:, 0:NT], NE0), ALU.mult))
            step(dve.tensor_tensor(lw[:, :, :], lw[:, :, :],
                                   nrm[:, NT:].rearrange("p (o e) -> p o e", o=1).to_broadcast([P, NT, NE0]), ALU.mult))
            step(dve.tensor_reduce(col[:, 0, :], lw[:, :, :], AX.X, ALU.max))
            step(dve.tensor_tensor(lg[:, :, :], lw[:, :, :], wide(col[:, 0, :], NE0), ALU.subtract))
            dve.wait_ge(s_fa, 3)
            step(dve.tensor_reduce(col[:, 1, :], lg[:, :, :], AX.X, ALU.add))
            step(dve.reciprocal(col[:, 1, :], col[:, 1, :]))
            step(dve.tensor_tensor(lg[:, :, :], lg[:, :, :], wide(col[:, 1, :], NE0), ALU.mult))
            step(dve.tensor_reduce(col[:, 2, :], lg[:, :, :], AX.X, ALU.max))
            step(dve.tensor_tensor(lw[:, :, :], lg[:, :, :], wide(col[:, 2, :], NE0), ALU.is_equal))
            step(dve.tensor_tensor(lw[:, :, :], lw[:, :, :],
                                   cst[:, C_FIRST:C_FIRST + NE0].rearrange("p (o e) -> p o e", o=1).to_broadcast([P, NT, NE0]),
                                   ALU.mult))
            step(dve.tensor_reduce(col[:, 3, :], lw[:, :, :], AX.X, ALU.max))
            dve.tensor_tensor(lw[:, :, :], lw[:, :, :], wide(col[:, 3, :], NE0), ALU.is_equal).then_inc(s_dne, 1)
            dve.wait_ge(s_dne, 3)
            step(dve.tensor_tensor(lw[:, :, :], lw[:, :, :], lg[:, :, :], ALU.mult))
            r0 = 0
            for e, r in enumerate(RANKS):
                i = dve.tensor_tensor(hg[:, :, r0:r0 + r], dn[:, :, PROJ + r0:PROJ + r0 + r],
                                      lw[:, :, e:e + 1].to_broadcast([P, NT, r]), ALU.mult)
                r0 += r
            step(i, False)
            for i in range(4):
                dve.wait_ge(s_fo, i + 1)
                xs = x[:, 4 * i:4 * i + 4, :].rearrange("p t d -> p (t d)")
                dve.tensor_tensor(xs, banks[:, i, :], xs, ALU.add).then_inc(s_fx, 1)

        PJ_AT, HI_AT = 17, 20
        SUM_AT, OUT_AT = 1, 13

        def setup1_pe(pe):
            pe.wait_ge(s_aw, 48)
            pe.wait_ge(ln[2]["xT"], 4)
            pe.matmul(banks[:, 4, 0:P], wvT[:, :], wkT[:, :], start=True, stop=True).then_inc(s_a1, 1)
            for n in range(NT):
                mm = pe.matmul(banks[:, n // 4, (n % 4) * P:(n % 4 + 1) * P], xT[:, n * P:(n + 1) * P], wkT[:, :], start=True, stop=True)
                if n % 4 == 3:
                    mm.then_inc(s_qt, 1)
            pe.wait_ge(s_a1m, 2)
            for g in range(GROUPS):
                mm = pe.matmul(banks[:, 5, g * P:(g + 1) * P], a1[:, g, :, :].rearrange("p h j -> p (h j)"), woT[:, :], start=True, stop=True)
            mm.then_inc(s_gg, 1)
            pe.wait_ge(s_gge, 1)
            pe.wait_ge(s_qte, 4)

        def setup1_act(act):
            for i in range(4):
                act.wait_ge(s_qt, i + 1)
                act.activation(qtm[:, 4 * i:4 * i + 4, :].rearrange("p t d -> p (t d)"), banks[:, i, :], ACT.Copy).then_inc(s_qte, 1)
            act.wait_ge(s_gg, 1)
            act.activation(gg[:, :, :].rearrange("p g d -> p (g d)"), banks[:, 5, :], ACT.Copy).then_inc(s_gge, 1)

        def setup1_dve(dve):
            dve.memset(a1[:, :, :, :].rearrange("p g h j -> p (g h j)"), 0.0).then_inc(s_a1m, 1)
            dve.memset(qv[:, :, :, :, :].rearrange("p b t h j -> p (b t h j)"), 0.0).then_inc(s_qv, 1)
            dve.wait_ge(s_qv, 1)
            dve.memset(qv[:, :, :, :, DK:DK + 1].rearrange("p b t h j -> p (b t h) j"), 1.0).then_inc(s_qv, 1)
            dve.wait_ge(s_a1m, 1)
            dve.wait_ge(s_a1, 1)
            bd = cst[:, C_BD:C_BD + P]
            dve.scalar_tensor_tensor(out=a1[:, :, :, 0:DK].rearrange("p g h j -> p (g h) j"),
                                     in0=banks[:, 4, 0:P].rearrange("p (h j) -> p h j", j=DK), scalar=SCALE1,
                                     in1=bd.rearrange("p (h j) -> p h j", j=DK), op0=ALU.mult, op1=ALU.mult).then_inc(s_a1m, 1)
            dve.wait_ge(s_qv, 2)
            dve.wait_ge(s_qte, 4)

        def prep1_pe(pe, u, b, g, first, part):
            if part == 0:
                pe.wait_ge(s_wk, 8 * (u - b) + 16)
                if not first:
                    pe.wait_ge(s_x1, 2 * (u - 1))
                for hf in range(2):
                    pe.matmul(banks[0:96, 6 + hf, :], wk3[:, :], xT[:, b * SEQ + hf * BLK:b * SEQ + (hf + 1) * BLK],
                              start=True, stop=True).then_inc(s_pj, 1)
            else:
                for hf in range(2):
                    pe.wait_ge(s_sq, 2 * u + hf + 1)
                    pe.matmul(banks[96:P, 6 + hf, :], cst[0:96, C_BLK:C_BLK + 32], sq1[:, hf * BLK:(hf + 1) * BLK],
                              start=True, stop=True).then_inc(s_nm, 1)

        def prep1_act(act, u, b, g, first, part):
            for hf in range(2):
                c = slice(hf * BLK, (hf + 1) * BLK)
                if part == 0:
                    act.wait_ge(s_pj, 2 * u + hf + 1)
                    act.activation(sq1[:, c], banks[0:96, 6 + hf, :], ACT.Square).then_inc(s_sq, 1)
                else:
                    act.wait_ge(s_nm, 2 * u + hf + 1)
                    act.activation(hi1[:, b, c], banks[:, 6 + hf, :], ACT.Copy).then_inc(s_hi, 1)

        def prep1_dve(dve, u, b, g, first, part):
            if part == 0:
                gs = g * GH * DK
                src = (qtm[:, b * TB:(b + 1) * TB, gs:gs + GH * DK] if isinstance(g, int) else
                       qtm[:, b * TB:(b + 1) * TB, bass.ds(gs, GH * DK)])
                if not isinstance(u, int) or u >= 2:
                    dve.wait_ge(s_pv1, 2 * TB * (u - 1))
                dve.tensor_scalar(qv[:, b, :, :, 0:DK], src.rearrange("p t (h k) -> p t h k", k=DK), 1.0, None, ALU.mult).then_inc(s_qv, 1)
                return
            cc = cst[:, C_COL:C_COL + 6]
            for hf in range(2):
                c = slice(hf * BLK, (hf + 1) * BLK)
                dve.wait_ge(s_hi, 2 * u + hf + 1)
                for k, t in enumerate((r1, l1)):
                    dve.tensor_scalar(t[:, b, c], hi1[:, b, c], cc[:, 3 * k + 1:3 * k + 2], cc[:, 3 * k + 2:3 * k + 3], ALU.mult, ALU.add)\
                       .then_inc(s_rl, 1)
                for k, t in enumerate((r1, l1)):
                    dve.wait_ge(s_rl, 8 * u + 4 * hf + k + 1)
                    dve.scalar_tensor_tensor(out=t[:, b, c], in0=banks[:, 6 + hf, :], scalar=cc[:, 3 * k:3 * k + 1], in1=t[:, b, c],
                                             op0=ALU.mult, op1=ALU.add).then_inc(s_rl, 1)
            dve.wait_ge(s_rl, 8 * u + 8)
            for h in range(GH):
                dve.tensor_scalar(l1h(b, h), l1[:, b, :], cst[:, C_MASK + h:C_MASK + h + 1], None, ALU.mult).then_inc(s_lh, 1)

        def slot1_pe(pe, u, b, j, first):
            t, h = divmod(j, GH)
            if j == 0:
                pe.wait_ge(s_lh, GH * (u + 1))
                pe.wait_ge(s_qv, u + 3)
            if not (first and j < 2):
                pe.wait_ge(s_exp1, NSLOT * u + j - 1)
            for sbk in range(2):
                mm = pe.matmul(banks[:, 2 * (j % 2) + sbk, :], l1h(b, h)[:, t * P:(t + 1) * P], r1[:, b, sbk * BLK:(sbk + 1) * BLK],
                               start=True, stop=True)
            mm.then_inc(s_st1, 1)
            if j % 2 and t > 0:
                pv1(pe, u, b, t - 1, h // 2, first)
            if j == NSLOT - 1:
                pv1(pe, u, b, t, 0, first)
                pv1(pe, u, b, t, 1, first)

        def pv1(pe, u, b, t, sbk, first):
            pe.wait_ge(s_exp1, NSLOT * u + GH * (t + 1))
            if t == 0 and not first:
                pe.wait_ge(s_zs, 2 * (u - 1) + sbk + 1)
            for h in range(GH):
                mm = pe.matmul(banks[32 * h:32 * h + 32, 4 + sbk, :], qv[:, b, t, h, :], pr[:, (GH * t + h) % NP1, sbk * BLK:(sbk + 1) * BLK],
                               start=(t == 0), stop=(t == TB - 1))
            mm.then_inc(s_pv1, 1)

        def slot1_act(act, u, b, j, first):
            t = j // GH
            act.wait_ge(s_st1, NSLOT * u + j + 1)
            if not (first and t < 2):
                act.wait_ge(s_pv1, 2 * TB * u + 2 * (t - 1))
            act.activation(pr[:, j % NP1, :], banks[:, 2 * (j % 2):2 * (j % 2) + 2, :].rearrange("p b c -> p (b c)"), ACT.Exp,
                           scale=2 * SCALE1).then_inc(s_exp1, 1)

        def sums1_pe(pe, u, b, g):
            for hf in range(2):
                pe.wait_ge(s_zs, 2 * u + hf + 1)
                if hf == 0:
                    pe.wait_ge(s_lh, GH * (u + 1))
                pe.matmul(banks[:, 6 + hf, :], cst[:, C_SEL:C_SEL + P], zs[:, hf * BLK:(hf + 1) * BLK], start=True, stop=True).then_inc(s_sum1, 1)

        def sums1_dve(dve, u, b, g):
            for hf in range(2):
                c = slice(hf * BLK, (hf + 1) * BLK)
                dve.wait_ge(s_pv1, 2 * TB * u + 2 * TB - 1 + hf)
                if not isinstance(u, int) or u > 0:
                    dve.wait_ge(s_zn, 2 * u)
                dve.tensor_copy(zs[:, c], banks[:, 4 + hf, :]).then_inc(s_zs, 1)
            for hf in range(2):
                c = slice(hf * BLK, (hf + 1) * BLK)
                dve.wait_ge(s_sum1, 2 * u + hf + 1)
                dve.reciprocal(rz[:, c], banks[:, 6 + hf, :]).then_inc(s_rz, 1)
                dve.wait_ge(s_rz, 2 * u + hf + 1)
                if not isinstance(u, int) or u > 0:
                    dve.wait_ge(s_op1, 2 * u)
                dve.tensor_tensor(zn[:, c], zs[:, c], rz[:, c], ALU.mult).then_inc(s_zn, 1)

        def out1_pe(pe, u, b, g):
            w = gg[:, g, :] if isinstance(g, int) else gg[:, bass.ds(g, 1), :].rearrange("p o d -> p (o d)")
            for hf in range(2):
                pe.wait_ge(s_zn, 2 * u + hf + 1)
                for t in range(4):
                    c = hf * BLK + t * P
                    mm = pe.matmul(banks[:, 6 + hf, t * P:(t + 1) * P], zn[:, c:c + P], w, start=True, stop=True)
                mm.then_inc(s_op1, 1)

        def out1_dve(dve, u, b, g):
            for hf in range(2):
                dve.wait_ge(s_op1, 2 * u + hf + 1)
                xs = x[:, b * TB + 4 * hf:b * TB + 4 * hf + 4, :].rearrange("p t d -> p (t d)")
                dve.tensor_tensor(xs, banks[:, 6 + hf, :], xs, ALU.add).then_inc(s_x1, 1)

        def attention1(e, prep, slot, sums, outp):
            prep(e, 0, 0, 0, True, 0)
            prep(e, 0, 0, 0, True, 1)

            def group(g, first, last):
                for b in range(BATCH):
                    u = 2 * g + b
                    f, l = first and b == 0, last and b == 1
                    for j in range(NSLOT):
                        slot(e, u, b, j, f)
                        if not l and j in (PJ_AT, HI_AT):
                            prep(e, u + 1, 1 - b, g + b, False, int(j == HI_AT))
                        if not f and j == SUM_AT:
                            sums(e, u - 1, 1 - b, g - 1 + b)
                        if not f and j == OUT_AT:
                            outp(e, u - 1, 1 - b, g - 1 + b)
            group(0, True, False)
            with e.Fori(1, GROUPS - 1) as g:
                group(g, False, False)
            group(GROUPS - 1, False, True)
            sums(e, 2 * GROUPS - 1, 1, GROUPS - 1)
            outp(e, 2 * GROUPS - 1, 1, GROUPS - 1)

        def gates_pe(pe):
            pe.wait_ge(s_mw, 48)
            pe.wait_ge(ln[3]["xT"], 4)
            for i in range(4):
                pe.matmul(banks[0:RH, i, :], wr[:, 0:RH], xT[:, i * BLK:(i + 1) * BLK], start=True, stop=True).then_inc(s_rh, 1)
            pe.wait_ge(s_rhe, 5)
            for n in range(NT):
                mm = pe.matmul(banks[:, 4, n * NE1:(n + 1) * NE1], rT[:, n * P:(n + 1) * P], wr2[:, :], start=True, stop=True)
            mm.then_inc(s_lo, 1)

        def gates_act(act):
            for i in range(4):
                act.wait_ge(s_rh, i + 1)
                act.activation(rT[0:RH, i * BLK:(i + 1) * BLK], banks[0:RH, i, :], ACT.Relu, bias=wr[0:RH, RH:RH + 1]).then_inc(s_rhe, 1)
            act.wait_ge(s_gc, 2)
            act.activation(ga[:, :, :], gl[:, :, :], ACT.Exp).then_inc(s_ga, 1)
            act.wait_ge(s_gc, 11)
            act.activation(col[:, 2, :], col[:, 2, :], ACT.Exp, scale=0.5).then_inc(s_ga, 1)

        def gates_dve(dve):
            done = [0]

            def step(ins):
                ins.then_inc(s_gc, 1)
                done[0] += 1
                dve.wait_ge(s_gc, done[0])

            def wide(t):
                return t.rearrange("p (n o) -> p n o", o=1).to_broadcast([P, NT, NE1])
            marks = cst[:, C_FIRST:C_FIRST + NE1].rearrange("p (o e) -> p o e", o=1).to_broadcast([P, NT, NE1])
            dve.memset(gw[:, :, 0:1].rearrange("p n o -> p (n o)"), 1.0).then_inc(s_gTe, 1)
            dve.wait_ge(s_lo, 1)
            lo = banks[:, 4, 0:NT * NE1].rearrange("p (n e) -> p n e", e=NE1)
            step(dve.tensor_reduce(col[:, 0, :], lo, AX.X, ALU.max))
            step(dve.tensor_tensor(gl[:, :, :], lo, wide(col[:, 0, :]), ALU.subtract))
            dve.wait_ge(s_ga, 1)
            step(dve.tensor_reduce(col[:, 1, :], ga[:, :, :], AX.X, ALU.add))
            step(dve.reciprocal(col[:, 1, :], col[:, 1, :]))
            step(dve.tensor_tensor(ga[:, :, :], ga[:, :, :], wide(col[:, 1, :]), ALU.mult))
            step(dve.tensor_reduce(col[:, 0, :], ga[:, :, :], AX.X, ALU.max))
            for k, oh in enumerate((oh1, oh2)):
                g = ga[:, :, :] if k == 0 else gl[:, :, :]
                m = col[:, 2 * k, :]
                dve.tensor_tensor(oh[:, :, :], g, wide(m), ALU.is_equal).then_inc(s_b2, 1)
                dve.wait_ge(s_b2, 3 * k + 1)
                dve.tensor_tensor(oh[:, :, :], oh[:, :, :], marks, ALU.mult).then_inc(s_b2, 1)
                dve.wait_ge(s_b2, 3 * k + 2)
                dve.tensor_reduce(col[:, 3, :], oh[:, :, :], AX.X, ALU.max).then_inc(s_b2, 1)
                dve.wait_ge(s_b2, 3 * k + 3)
                step(dve.tensor_tensor(oh[:, :, :], oh[:, :, :], wide(col[:, 3, :]), ALU.is_equal))
                if k == 0:
                    step(dve.scalar_tensor_tensor(out=gl[:, :, :], in0=oh[:, :, :], scalar=-4.0, in1=ga[:, :, :],
                                                  op0=ALU.mult, op1=ALU.add))
                    step(dve.tensor_reduce(col[:, 2, :], gl[:, :, :], AX.X, ALU.max))
            step(dve.tensor_tensor(col[:, 2, :], col[:, 2, :], col[:, 0, :], ALU.subtract))
            dve.wait_ge(s_ga, 2)
            step(dve.tensor_scalar(col[:, 1, :], col[:, 2, :], 1.0, None, ALU.add))
            step(dve.reciprocal(col[:, 1, :], col[:, 1, :]))
            step(dve.tensor_tensor(col[:, 2, :], col[:, 2, :], col[:, 1, :], ALU.mult))
            step(dve.tensor_tensor(oh1[:, :, :], oh1[:, :, :], wide(col[:, 1, :]), ALU.mult))
            step(dve.tensor_tensor(oh2[:, :, :], oh2[:, :, :], wide(col[:, 2, :]), ALU.mult))
            step(dve.tensor_tensor(gw[:, :, 1:], oh1[:, :, :], oh2[:, :, :], ALU.add))
            for i in range(4):
                dve.wait_ge(s_gT, i + 1)
                dve.tensor_copy(gwT[:, i * BLK:(i + 1) * BLK], banks[0:1 + NE1, 6 + i % 2, :]).then_inc(s_gTe, 1)
            for i in range(4):
                dve.wait_ge(s_b2, 7 + i)
                xs = x[:, 4 * i:4 * i + 4, :].rearrange("p t d -> p (t d)")
                dve.tensor_tensor(xs, banks[:, 6 + i % 2, :], xs, ALU.add).then_inc(s_xe, 1)

        def bias_pe(pe):
            pe.wait_ge(s_gc, 17)
            pe.wait_ge(s_gTe, 1)
            for i in range(4):
                if i >= 2:
                    pe.wait_ge(s_gTe, i)
                for t in range(4):
                    n = 4 * i + t
                    mm = pe.transpose(banks[0:1 + NE1, 6 + i % 2, t * P:(t + 1) * P], gw[:, n, :], ident)
                mm.then_inc(s_gT, 1)
            for i in range(4):
                pe.wait_ge(s_gTe, 5)
                if i >= 2:
                    pe.wait_ge(s_xe, i - 1)
                for t in range(4):
                    n = 4 * i + t
                    mm = pe.matmul(banks[:, 6 + i % 2, t * P:(t + 1) * P], gwT[:, n * P:(n + 1) * P], b2[:, :], start=True, stop=True)
                mm.then_inc(s_b2, 1)

        def up_pe(pe, q, w, tb, first):
            k = 4 * q + tb
            if tb == 0:
                pe.wait_ge(s_ew[w], 8 * (q - w) + 16)
            for i in range(NI):
                if not (first and tb == 0):
                    pe.wait_ge(s_hid, NI * (k - 1) + i + 1)
                pe.matmul(banks[:, i, :], w1[:, w, i * P:(i + 1) * P], xT[:, tb * BLK:(tb + 1) * BLK], start=True, stop=True).then_inc(s_up, 1)

        def down_pe(pe, q, w, tb, first):
            k = 4 * q + tb
            pe.wait_ge(s_hid, NI * (k + 1))
            if not (first and tb < 2):
                pe.wait_ge(s_xe, 4 + k - 1)
            for t in range(4):
                for i in range(NI):
                    mm = pe.matmul(banks[:, 4 + tb % 2, t * P:(t + 1) * P], hid[:, tb % 2, i, t * P:(t + 1) * P],
                                   w1[:, w, INNER + i * P:INNER + (i + 1) * P], start=(i == 0), stop=(i == NI - 1))
            mm.then_inc(s_down, 1)

        def expert_act(act, q, w, tb, first):
            k = 4 * q + tb
            for i in range(NI):
                act.wait_ge(s_up, NI * k + i + 1)
                if i == 0 and not (first and tb < 2):
                    act.wait_ge(s_down, k - 1)
                act.activation(hid[:, tb % 2, i, :], banks[:, i, :], ACT.Silu, bias=w1[:, w, 2 * INNER + i:2 * INNER + i + 1]).then_inc(s_hid, 1)

        def expert_dve(dve, q, w, tb, first):
            k = 4 * q + tb
            dve.wait_ge(s_down, k + 1)
            for t in range(4):
                n = 4 * tb + t
                g = gw[:, n, q:q + 1] if isinstance(q, int) else gw[:, n, bass.ds(q, 1)]
                i = dve.scalar_tensor_tensor(out=x[:, n, :], in0=banks[:, 4 + tb % 2, t * P:(t + 1) * P], scalar=g, in1=x[:, n, :],
                                             op0=ALU.mult, op1=ALU.add)
            i.then_inc(s_xe, 1)

        def experts(e, head, tail):
            def expert(q, w, first):
                for tb in range(4):
                    head(e, q, w, tb, first)
                    if not (first and tb == 0):
                        tail(e, q if tb else q - 1, w if tb else 1 - w, (tb - 1) % 4, first)
            expert(0, 0, True)
            with e.Fori(0, NE1 // 2) as m:
                expert(2 * m + 1, 1, False)
                expert(2 * m + 2, 0, False)
            tail(e, NE1, 0, 3, False)

        def x_out(e):
            e.wait_ge(s_xe, 4 + 4 * (1 + NE1))
            e.dma_start(out, x[:, :, :]).then_inc(s_out, 16)
            e.wait_ge(s_out, 16)

        @block.sync
        def _(sp):
            for i in range(4):
                sp.dma_start(x[:, 4 * i:4 * i + 4, :], a["x"][:, 4 * i:4 * i + 4, :]).then_inc(s_x[i], 16)
            sp.dma_start(cst[:, :], a["cst"]).then_inc(s_const, 16)
            sp.dma_start(wqkv[:, :], a["wqkv"][0]).then_inc(s_wq, 16)
            sp.dma_start(wpr[:, :, :], a["wpr"]).then_inc(s_wp, 16)
            sp.dma_start(mD[:, :, :, :].rearrange("r h s c -> r (h s c)"), a["mD"]).then_inc(s_maskd, 16)
            for p in range(1, PAIRS):
                sp.wait_ge(s_v, 4 * p)
                sp.wait_ge(s_qk_lo, 8 * p)
                sp.dma_start(wqkv[:, :], a["wqkv"][p]).then_inc(s_wq, 16)
            sp.dma_start(wdn[:, :], a["wdn"]).then_inc(s_fw, 16)
            sp.dma_start(wbase[:, :], a["wbase"]).then_inc(s_fw, 16)
            sp.dma_start(wup[:, :], a["wup"]).then_inc(s_fw, 16)
            sp.dma_start(small[:, :], a["small"]).then_inc(s_fw, 16)
            for t, n in ((wkT, "wkT"), (wvT, "wvT"), (woT, "woT")):
                sp.dma_start(t[:, :], a[n]).then_inc(s_aw, 16)
            sp.dma_start(wk3[:, :], a["wk3"][0]).then_inc(s_wk, 16)
            for t, n in ((wr, "wr"), (wr2, "wr2"), (b2, "b2")):
                sp.dma_start(t[:, :], a[n]).then_inc(s_mw, 16)
            for q in range(2):
                sp.dma_start(w1[:, q, :], a["experts"][q]).then_inc(s_ew[q], 16)
            for g in range(1, GROUPS):
                sp.wait_ge(s_pj, 4 * g)
                sp.dma_start(wk3[:, :], a["wk3"][g]).then_inc(s_wk, 16)
            for q in range(2, 1 + NE1):
                sp.wait_ge(s_down, 4 * (q - 1))
                sp.wait_ge(s_hid, 4 * NI * (q - 1))
                sp.dma_start(w1[:, q % 2, :], a["experts"][q]).then_inc(s_ew[q % 2], 16)
            x_out(sp)

        @block.gpsimd
        def _(pool):
            pool.memset(zero[:, :], 0.0).then_inc(s_setup, 1)
            pool.wait_ge(s_setup, N_SETUP)

            def padd(e, u, b, j, first):
                h, sbk, t, o = unit(j)
                if t == 0 and h == 0 and not first:
                    e.wait_ge(s_sum, 2 * u + sbk - 1)
                elif t > 0:
                    e.wait_ge(s_padd, NU * u + j - 1)
                e.wait_ge(s_exp, NU * u + j + 1)
                src = zero[:, :] if t == 0 else pacc[:, sbk, h, o:BLK]
                e.tensor_tensor(pacc[:, sbk, h, o:BLK], src, pr[:, j % NP0, 0:BLK - o], ALU.add).then_inc(s_padd, 1)
            no = lambda *_: None
            attention0(pool, no, padd, no, no, no)

        @block.scalar
        def _(act):
            ln_act(act, 0)

            def prep(e, u, b, n, first):
                for k in range(NITEM) if n is None else [n]:
                    act_item(e, u, b, k)

            def exps(e, u, b, j, first):
                h, sbk, t, o = unit(j)
                e.wait_ge(s_st, NU * u + j + 1)
                if not (first and j < NP0):
                    e.wait_ge(s_pv, NU * u + j - NP0 + 1)
                    e.wait_ge(s_padd, NU * u + j - NP0 + 1)
                e.activation(pr[:, j % NP0, 0:BLK - o], banks[:, j % 3, 0:BLK - o], ACT.Exp, scale=SCALE0).then_inc(s_exp, 1)
            no = lambda *_: None
            attention0(act, prep, exps, no, no, no)
            ln_act(act, 1)
            linear_act(act)
            ln_act(act, 2)
            setup1_act(act)
            attention1(act, prep1_act, slot1_act, no, no)
            ln_act(act, 3)
            gates_act(act)
            experts(act, expert_act, no)

        @block.vector
        def _(dve):
            dve.memset(ones[:, :], 1.0).then_inc(s_setup, 1)
            dve.memset(kb[DH:KB_ROWS, :, :, :].bitcast(F32).rearrange("p b h s -> p (b h s)"), 1.0).then_inc(s_setup, 1)
            dve.memset(mx2[:, :, :], 0.0).then_inc(s_setup, 1)
            ln_dve(dve, 0, lambda e, n: e.wait_ge(s_x[n // 4], 16) if n % 4 == 0 else None)
            dve.wait_ge(s_const, 16)
            for o, c in ((idb, C_ID), (msb, C_MS), (mtb, C_MT)):
                dve.tensor_copy(o[:, :], cst[:, c:c + P]).then_inc(s_setup, 1)

            def prep(e, u, b, n, first):
                if n is None:
                    e.wait_ge(s_maskd, 16)
                for k in range(NITEM) if n is None else [n]:
                    dve_item(e, u, b, k, first)
            no = lambda *_: None
            attention0(dve, prep, no, dve_norm, dve_acc, no)
            dve.memset(hg[:, :, RSUM:RSUM + 1].rearrange("p n o -> p (n o)"), 0.0)
            ln_dve(dve, 1, lambda e, n: e.wait_ge(s_xacc, 2 * PAIRS) if n == 0 else None)
            linear_dve(dve)
            ln_dve(dve, 2, lambda e, n: e.wait_ge(s_fx, n // 4 + 1) if n % 4 == 0 else None)
            setup1_dve(dve)
            attention1(dve, prep1_dve, no, sums1_dve, out1_dve)
            dve.memset(rT[RH:RH + 1, :], 1.0).then_inc(s_rhe, 1)
            ln_dve(dve, 3, lambda e, n: e.wait_ge(s_x1, 4 * GROUPS) if n == 0 else None)
            gates_dve(dve)
            experts(dve, no, expert_dve)

        @block.tensor
        def _(pe):
            pe.wait_ge(s_const, 16)
            ln_pe(pe, 0)
            pe.wait_ge(ln[0]["xT"], 4)
            pe.wait_ge(s_setup, N_SETUP)
            pe.wait_ge(s_wp, 16)

            def prep(e, u, b, n, first):
                for k in range(NITEM) if n is None else [n]:
                    pe_item(e, u, b, k, first)

            def rest(e, u, b, j, first):
                if j >= 2:
                    pe_pv(e, u, b, j - 2, first)
                if j == NU - 1:
                    pe_pv(e, u, b, j - 1, first)
                    pe_pv(e, u, b, j, first)
            attention0(pe, prep, lambda e, u, b, j, f: pe_scores(e, u, b, j), lambda e, u, b, sbk, f: pe_sums(e, u, sbk, f), pe_out, rest)
            ln_pe(pe, 1)
            linear_pe(pe)
            ln_pe(pe, 2)
            setup1_pe(pe)
            attention1(pe, prep1_pe, slot1_pe, sums1_pe, out1_pe)
            ln_pe(pe, 3)
            gates_pe(pe)
            bias_pe(pe)
            experts(pe, up_pe, down_pe)


def kernel(**inp):
    import concourse.bacc as bacc
    from concourse.bass_utils import run_bass_kernel_spmd

    f = {k: np.ascontiguousarray(t) for k, t in inp.items()}

    def pairs(w):
        return w.reshape(PAIRS, 2 * DH, D).transpose(0, 2, 1)

    def rows(b):
        return b.reshape(PAIRS, 2 * DH, 1)

    cst, m = constants()
    arrays = {
        "x": f["L0_attn_x"].reshape(NT, P, D).transpose(1, 0, 2),
        "cst": cst,
        "mD": m,
        "wqkv": np.concatenate([pairs(f["L0_attn_Wq"]), pairs(f["L0_attn_Wk"]), pairs(f["L0_attn_Wv"]),
                                np.broadcast_to(f["L0_attn_bv"].reshape(PAIRS, 1, D), (PAIRS, P, D)),
                                rows(f["L0_attn_bq"]), rows(f["L0_attn_bk"])], axis=2),
        "wpr": f["L0_attn_proj"].reshape(TB, P, D).transpose(1, 0, 2),
    }
    ranks = range(NE0)
    zeros = np.zeros((1, D), np.float32)
    arrays |= {
        "wdn": np.concatenate([f["L0_ffn_Wp"]] + [f[f"L0_ffn_Wd{i}"] for i in ranks] + [zeros]).T,
        "wbase": f["L0_ffn_W"].T,
        "wup": np.concatenate([f[f"L0_ffn_Wu{i}"].T for i in ranks] + [zeros]),
        "small": np.broadcast_to(np.concatenate([f["L0_ffn_bp"], f["L0_ffn_sim"].T.reshape(-1), f["L0_ffn_temp"]]),
                                 (P, PROJ + NE0 * PROJ + 1)),
        "wkT": f["L1_attn_W_k"].T,
        "wvT": f["L1_attn_W_v"].T,
        "woT": f["L1_attn_W_o"].T,
        "wk3": np.stack([np.tile(w.T, (1, 3)) for w in f["L1_attn_W_k"].reshape(GROUPS, GH * DK, D)]),
        "wr": np.concatenate([f["L1_ffn_Wr1"], np.resize(f["L1_ffn_br1"], (P, 1))], axis=1),
        "wr2": np.concatenate([f["L1_ffn_Wr2"], f["L1_ffn_br2"][None]]),
        "b2": np.concatenate([f["L1_ffn_bs2"][None], f["L1_ffn_be2"]]),
        "experts": np.stack([np.concatenate([up, down.reshape(NI, P, D).transpose(1, 0, 2).reshape(P, INNER), bias.reshape(NI, P).T],
                                            axis=1)
                             for up, down, bias in zip([f["L1_ffn_Ws1"], *f["L1_ffn_We1"]], [f["L1_ffn_Ws2"], *f["L1_ffn_We2"]],
                                                       [f["L1_ffn_bs1"], *f["L1_ffn_be1"]])]),
    }
    arrays = {k: np.ascontiguousarray(t) for k, t in arrays.items()}
    nc = bacc.Bacc("TRN2", target_bir_lowering=False, num_devices=1)
    a = {k: nc.dram_tensor(f"in_{k}", t.shape, F32, kind="ExternalInput").ap() for k, t in arrays.items()}
    out = nc.dram_tensor("out", (P, NT, D), F32, kind="ExternalOutput").ap()
    build_kernel(nc, a, out, None)
    r = run_bass_kernel_spmd(nc, [{f"in_{k}": t for k, t in arrays.items()}], core_ids=[0])
    y = np.asarray(r.results[0]["out"]).reshape(P, NT, D)
    return np.ascontiguousarray(y.transpose(1, 0, 2)).reshape(BATCH, SEQ, D)
```

```python
import math
from contextlib import ExitStack

import numpy as np

import concourse.bass as bass
from concourse import mybir

F32, F32R, BF16 = mybir.dt.float32, mybir.dt.float32r, mybir.dt.bfloat16
ACT, ALU, AX = mybir.ActivationFunctionType, mybir.AluOpType, mybir.AxisListType

P = 128
BATCH, SEQ, D = 2, 1024, 128
TOK = BATCH * SEQ
NT, TB = TOK // P, SEQ // P
BLK = 512
EPS = 1e-5

HEADS, DH = 16, 64
PAIRS = HEADS // 2
SCALE0 = 1.0 / math.sqrt(DH)
MROWS = 2 * TB
KB_ROWS = DH + MROWS
UNITS = [(0, t) for t in range(TB // 2)] + [(1, t) for t in range(TB)]
NU = 2 * len(UNITS)
SB0_UNITS = TB
PIECES = [(h, s, c, min(BLK, P * (s + 1) - c)) for half in range(2) for h in range(2) for s in range(half * TB // 2, (half + 1) * TB // 2)
          for c in range(0, P * (s + 1), BLK)]
NPIECE = len(PIECES)
NPIECE0 = TB
NP0 = 8
NCH = BLK // P
RROWS = 2 * 2 * NCH
NEG = -1e30

PROJ, RANKS = 32, (1, 2, 4, 8)
NE0, RSUM = len(RANKS), sum(RANKS)
DOWN = PROJ + RSUM + 1
CLAMP = float(np.log(1.0 / 0.01))

DK = 8
GH = 4
GROUPS = HEADS // GH
SCALE1 = 1.0 / math.sqrt(DK)
NSLOT = GH * TB
NP1 = 8

INNER, NE1 = 512, 8
NI = INNER // P
RH = D // 4
GROWS = 2 * (1 + NE1)

C_ID, C_MS, C_MT, C_SEL, C_BD, C_BLK, C_COL = 0, 128, 256, 384, 512, 640, 672
C_MASK = C_COL + 6
C_FIRST = C_MASK + GH
C_SPR = C_FIRST + NE1
C_EXP = C_SPR + P
CONSTS = C_EXP + 1 + NE1


def constants():
    c = np.zeros((P, CONSTS), np.float32)
    i = np.arange(P)
    c[:, C_ID:C_ID + P] = np.eye(P)
    c[:, C_MS:C_MS + P] = np.where(i[None, :] > i[:, None], NEG, 0)
    c[:, C_MT:C_MT + P] = np.where(i[None, :] < i[:, None], NEG, 0)
    c[:, C_SEL:C_SEL + P] = i[:, None] == i[None, :] // 32 * 32 + DK
    c[:, C_BD:C_BD + P] = i[:, None] // DK == i[None, :] // DK
    c[:32, C_BLK:C_BLK + 32] = -0.5 * (i[:32, None] // DK == i[None, :32] // DK)
    quad, j = i // 32, i % DK
    hi, lo, one = (0, 1, 0), (1, -1, 0), (0, 0, 1)
    for p in range(P):
        r = [hi, lo, hi][quad[p]] if quad[p] < 3 else {0: hi, 1: lo, 2: one, 3: one}.get(j[p], (0, 0, 0))
        l = [hi, hi, lo][quad[p]] if quad[p] < 3 else {0: one, 1: one, 2: hi, 3: lo}.get(j[p], (0, 0, 0))
        c[p, C_COL:C_COL + 3], c[p, C_COL + 3:C_COL + 6] = r, l
        c[p, C_MASK + p % 32 // DK] = 1
    c[:, C_FIRST:C_FIRST + NE1] = np.arange(NE1, 0, -1)
    c[:RROWS, C_SPR:C_SPR + P] = i[:RROWS, None] // NCH % 2 == i[None, :] // DH
    c[:GROWS, C_EXP:C_EXP + 1 + NE1] = i[:GROWS, None] % (1 + NE1) == np.arange(1 + NE1)
    mr = np.zeros((RROWS, NCH, P), np.float32)
    for r in range(RROWS):
        mr[r, r % NCH] = 1
    m = np.zeros((MROWS, 2, TB, P), np.float32)
    for h in range(2):
        for s in range(TB):
            m[h * TB + s, h, s] = 1
    pick = np.zeros((HEADS, TB, 2, DH), np.float32)
    for h in range(HEADS):
        pick[h, h // 2, h % 2] = 1
    return c, mr, m.reshape(MROWS, 2 * SEQ), pick.reshape(HEADS, TB, P)


def build_kernel(nc, a, out, stop):
    ctx = ExitStack()
    with ctx:
        def sb(name, shape, dt=F32):
            return ctx.enter_context(nc.sbuf_tensor(name, shape, dt))

        def sem(name):
            return ctx.enter_context(nc.semaphore(name))

        x = sb("x", [P, NT, D])
        xn = sb("xn", [P, NT, D])
        xT = sb("xT", [P, TOK])
        cst = sb("cst", [P, CONSTS])
        mD = sb("mD", [MROWS, 2, TB, P])
        idb = sb("idb", [P, P], BF16)
        msb = sb("msb", [P, P], BF16)
        mtb = sb("mtb", [P, P], BF16)
        mR = sb("mR", [RROWS, NCH, P])
        spr = sb("spr", [RROWS, P], F32R)
        ones = sb("ones", [P, 2])
        st = sb("st", [P, NT, 6])
        mv = sb("mv", [P, NT, 2])
        rs = sb("rs", [P, 4, NT])

        qa = sb("qa", [P, BATCH, 2, SEQ], F32R)
        qb = sb("qb", [P, BATCH, 2, SEQ], F32R)
        ka = sb("ka", [P, BATCH, 2, SEQ], F32R)
        kb = sb("kb", [P, BATCH, 2, SEQ], F32R)
        v = sb("v", [P, BATCH, TB, D])
        wqkv = sb("wqkv", [P, 3 * D + 2])
        wpr = sb("wpr", [P, TB, D])
        pr = sb("pr", [P, NP1, SEQ])
        pacc = sb("pacc", [P, 2, 2, BLK])
        zero = sb("zero", [P, BLK])
        mx = sb("mx", [P, 2, TB])
        mx2 = sb("mx2", [P, 2, TB // 2])
        bv2 = sb("bv2", [P, HEADS])
        cb = sb("cb", [HEADS, D])
        pick = sb("pick", [HEADS, TB, P])
        rcp = sb("rcp", [P, 3, 2 * NCH], F32R)
        rows2 = sb("rows2", [GROWS, 2, BLK], F32R)
        rex = rows2[0:RROWS, 0, :].rearrange("r (c q) -> r c q", c=NCH)
        rall = sb("rall", [P, BLK])
        zz = sb("zz", [P, 2, SEQ // 2])

        wdn = sb("wdn", [P, DOWN])
        wbase = sb("wbase", [P, D])
        wup = sb("wup", [RSUM + 1, D])
        small = sb("small", [P, PROJ + NE0 * PROJ + 1])
        dn = sb("dn", [P, NT, DOWN])
        pj = sb("pj", [P, NT, PROJ])
        sq = zero[:, :].rearrange("p (n k) -> p n k", n=NT)
        prod = xn[:, :, :].rearrange("p n (e k) -> p n e k", e=NE0)
        simq = sb("simq", [P, NE0, PROJ])
        nrm = sb("nrm", [P, NT + NE0])
        escale = sb("escale", [P, 1])
        lg = sb("lg", [P, NT, NE0])
        lw = sb("lw", [P, NT, NE0])
        col = sb("col", [P, 4, NT])
        hg = sb("hg", [P, NT, RSUM + 1])
        hgT = mD[:, :, :, :].rearrange("r h s c -> r (h s c)")

        r1 = qa[:, :, 0, :]
        hi1 = qa[:, :, 1, :]
        l1 = qb[:, :, 0, :]

        def l1h(b, h):
            return (ka, kb)[h // 2][:, b, h % 2, :]
        wk3 = sb("wk3", [P, 3 * GH * DK])
        wkT = sb("wkT", [P, D])
        wvT = sb("wvT", [P, D])
        woT = sb("woT", [P, D])
        a1 = sb("a1", [P, GROUPS, GH, 32])
        gg = sb("gg", [P, GROUPS, D])
        qtm = xn
        qv = v[:, :, :, :].rearrange("p b t (h j) -> p b t h j", j=32)
        sq1 = sb("sq1", [3 * GH * DK, SEQ])
        zs = pacc[:, 0, :, :].rearrange("p h c -> p (h c)")
        rz = pacc[:, 1, :, :].rearrange("p h c -> p (h c)")
        zn = zz[:, :, :].rearrange("p h c -> p (h c)")

        w1 = sb("w1", [P, 2, 2 * INNER + NI])
        b2 = sb("b2", [GROWS, D])
        wr = sb("wr", [P, RH + 1])
        wr2 = sb("wr2", [RH + 1, NE1])
        rT = pacc[0:RH + 1, :, :, :].rearrange("p k h c -> p (k h c)")
        gl = sb("gl", [P, NT, NE1])
        ga = sb("ga", [P, NT, NE1])
        oh1 = sb("oh1", [P, NT, NE1])
        oh2 = sb("oh2", [P, NT, NE1])
        gw = sb("gw", [P, NT, 1 + NE1])
        gw2 = sb("gw2", [P, NT, 2, 1 + NE1], F32R)
        gT = v[0:GROWS, :, :, :].rearrange("p b t d -> p (b t d)")
        gsel = rows2
        onesr = sb("onesr", [GROWS, P], F32R)
        flat = lambda t: t[:, :, :, :].rearrange("p b h s -> p (b h s)")
        x2 = flat(qa).rearrange("p (k s) -> p k s", k=2)
        w2 = flat(kb).rearrange("p (w k s) -> p w k s", w=2, k=2)
        act2 = [flat(t).rearrange("p (b i s) -> p b i s", b=2, i=NI) for t in (qb, ka)]
        hid = pr[:, 0:4, :].rearrange("p (b i) (k c) -> p b (i k) c", b=2, k=2)
        yT = pr[:, 4:6, :].rearrange("p b (k c) -> p (b k) c", k=2)

        banks = ctx.enter_context(nc.psum_tensor("banks", [P, 8, BLK], F32))

        ident = cst[:, C_ID:C_ID + P]
        block = ctx.enter_context(nc.Block())

        s_x = [sem(f"x_in{i}") for i in range(4)]
        s_const, s_maskd = sem("const_in"), sem("maskd_in")
        s_wq, s_wp = sem("wqkv_in"), sem("wproj_in")
        s_out = sem("out_done")
        s_setup = sem("setup_done")
        N_SETUP = 8
        ln = [{n: sem(f"ln{k}_{n}") for n in ("stats", "aggr", "ln", "rstd", "newton", "norm", "turned", "xT")} for k in range(4)]
        s_prep_qk, s_prep_v, s_prep_m, s_prep_t = sem("qk_projected"), sem("v_projected"), sem("piece_scored"), sem("max_turned")
        s_qk_hi, s_qk_lo, s_v = sem("qk_hi_done"), sem("qk_lo_done"), sem("v_stored")
        s_pmax, s_mneg, s_mrow = sem("piece_max"), sem("max_negated"), sem("max_rows")
        s_st, s_exp, s_padd, s_pv = sem("scored"), sem("exp_done"), sem("prob_added"), sem("pv_done")
        s_sum, s_rcp, s_rt, s_rex, s_spread = (sem(n) for n in ("sums_done", "sums_inverted", "recip_turned", "recip_in_columns", "recip_spread"))
        s_rall = sem("recip_stored")
        s_zz, s_op, s_xacc = sem("z_ready"), sem("out_projected"), sem("x_added")

        s_cb, s_cbe = sem("bias_rows"), sem("bias_added")
        s_fw = sem("linear_weights_in")
        s_dn, s_dne, s_ch, s_fa, s_hT, s_hTe, s_fo, s_fx = (sem(n) for n in (
            "down_projected", "down_stored", "router_chain", "router_act", "gated_turned", "gated_stored", "linear_done", "linear_added"))
        s_aw, s_wk = sem("attn1_weights_in"), sem("wk3_in")
        s_a1, s_a1m, s_gg, s_gge, s_qt, s_qte = (sem(n) for n in (
            "merged_done", "merged_masked", "merged_wo_done", "merged_wo_stored", "qtm_done", "qtm_stored"))
        s_pj, s_sq, s_nm, s_hi, s_rl, s_lh, s_qv = (sem(n) for n in (
            "q_projected", "q_squared", "norms_done", "q_rounded", "sides_filled", "heads_masked", "qv_filled"))
        s_st1, s_exp1, s_pv1, s_zs, s_sum1, s_rz, s_zn, s_op1, s_x1 = (sem(n) for n in (
            "dist_scored", "dist_exp", "dist_pv", "ctx_stored", "ctx_sums", "ctx_recip", "ctx_ready", "ctx_projected", "attn1_added"))
        s_xs, s_ws, s_gs, s_spreadg, s_gh, s_hh, s_hl, s_yT, s_y = (sem(n) for n in (
            "x_split", "weights_split", "gates_selected", "gates_spread", "act_weighted", "act_rounded", "act_split", "sums_stored", "sums_turned"))
        s_mw, s_ew = sem("moe_weights_in"), [sem("expert_in0"), sem("expert_in1")]
        s_rh, s_rhe, s_lo, s_gc, s_ga, s_gT, s_gTe, s_b2, s_up, s_hid, s_down, s_xe = (sem(n) for n in (
            "router_hidden", "router_relu", "router_logits", "gate_chain", "gate_act", "gates_turned", "gates_stored", "bias_done",
            "up_done", "silu_done", "down_done", "expert_added"))

        def ln_dve(v_, k, ready):
            s = ln[k]
            for n in range(NT):
                ready(v_, n)
                v_.bn_stats(out=st[:, n, :], in_=x[:, n, :]).then_inc(s["stats"], 1)
            v_.wait_ge(s["stats"], NT)
            for n in range(NT):
                v_.bn_aggr(out=mv[:, n, :], in_=st[:, n, :]).then_inc(s["aggr"], 1)
            v_.wait_ge(s["aggr"], NT)
            v_.tensor_scalar(rs[:, 0, :], mv[:, :, 1], EPS, None, ALU.add).then_inc(s["aggr"], 1)
            v_.wait_ge(s["rstd"], 1)
            v_.tensor_tensor(rs[:, 3, :], rs[:, 2, :], rs[:, 2, :], ALU.mult).then_inc(s["newton"], 1)
            v_.wait_ge(s["newton"], 1)
            v_.tensor_tensor(rs[:, 3, :], rs[:, 3, :], rs[:, 0, :], ALU.mult).then_inc(s["newton"], 1)
            v_.wait_ge(s["newton"], 2)
            v_.tensor_scalar(rs[:, 3, :], rs[:, 3, :], -0.5, 1.5, ALU.mult, ALU.add).then_inc(s["newton"], 1)
            v_.wait_ge(s["newton"], 3)
            v_.tensor_tensor(rs[:, 3, :], rs[:, 3, :], rs[:, 2, :], ALU.mult).then_inc(s["newton"], 1)
            v_.wait_ge(s["newton"], 4)
            for n in range(NT):
                v_.tensor_scalar(xn[:, n, :], x[:, n, :], mv[:, n, 0:1], rs[:, 3, n:n + 1],
                                 ALU.subtract, ALU.mult).then_inc(s["norm"], 1)

        def ln_act(act, k):
            s = ln[k]
            act.wait_ge(s["aggr"], NT + 1)
            act.activation(rs[:, 1, :], rs[:, 0, :], ACT.Ln).then_inc(s["ln"], 1)
            act.wait_ge(s["ln"], 1)
            act.activation(rs[:, 2, :], rs[:, 1, :], ACT.Exp, scale=-0.5).then_inc(s["rstd"], 1)
            for i in range(4):
                act.wait_ge(s["turned"], i + 1)
                act.activation(xT[:, i * BLK:(i + 1) * BLK], banks[:, i, :], ACT.Copy).then_inc(s["xT"], 1)

        def ln_pe(pe, k):
            s = ln[k]
            for i in range(4):
                pe.wait_ge(s["norm"], 4 * i + 4)
                for j in range(4):
                    mm = pe.transpose(banks[:, i, j * P:(j + 1) * P], xn[:, 4 * i + j, :], ident)
                mm.then_inc(s["turned"], 1)

        QK_AT, V_AT, TURN_AT = [0, 3, 6, 10], [2, 4], 21
        MAX_AT = [7, 8, 9, 9, 10, 11, 11, 12, 13, 13, 14, 14, 15, 15, 16, 16, 16, 16, 17, 17, 18, 18, 19, 19]
        SHARED = 7
        PREP_AT = {}
        for kind, at in (("qk", QK_AT), ("v", V_AT), ("max", MAX_AT), ("turn", [TURN_AT])):
            for k, slot in enumerate(at):
                own = {"qk": 3, "v": 7, "max": 7 if k < SHARED or k % 2 else 3, "turn": 3}[kind]
                PREP_AT.setdefault(slot, []).append((kind, k, own))
        AT_NUMBER, ITEMS = {}, []
        for slot in sorted(PREP_AT):
            AT_NUMBER[slot] = list(range(len(ITEMS), len(ITEMS) + len(PREP_AT[slot])))
            ITEMS += PREP_AT[slot]
        NITEM = len(ITEMS)
        DVE_LATER = 2

        def shares(engine):
            at = {}
            for slot, numbers in AT_NUMBER.items():
                for n in numbers:
                    qk = ITEMS[n][0] == "qk"
                    for h in (0, 1) if qk and engine != "pe" else (0,):
                        later = {"pe": 0, "act": h, "dve": DVE_LATER + h}[engine] if qk else 0
                        at.setdefault(slot + later, []).append((not qk, n, h))
            return {slot: [(n, h) for _, n, h in sorted(at[slot])] for slot in at}
        TAIL0_AT, TAIL1_AT, OUT0_AT = (12, 14, 16), (2, 4, 5), 8

        def ends(engine):
            at = {}
            for back, sbk, slots in ((0, 0, TAIL0_AT), (1, 1, TAIL1_AT + (OUT0_AT,))):
                for stage, slot in enumerate(slots):
                    at.setdefault(slot + TAIL_LATER[engine][stage], []).append((back, sbk, stage))
            return at
        TAIL_LATER = {"pe": (0, 0, 0, 0), "act": (0, 0, 0, 0), "dve": (1, 1, 1, 2)}

        def pbank(n):
            return banks[:, ITEMS[n][2], :]

        def wait_bank(e, u, n, first):
            before = [i for i in range(n) if ITEMS[i][2] == ITEMS[n][2]]
            if not before and first:
                return
            i = before[-1] if before else max(i for i in range(NITEM) if ITEMS[i][2] == ITEMS[n][2])
            kind, k, _ = ITEMS[i]
            s, per, k = {"qk": (s_qk_lo, 8, 2 * k + 1), "v": (s_v, 2, k), "max": (s_pmax, NPIECE, k), "turn": (s_mrow, 2, 1)}[kind]
            e.wait_ge(s, (u if before else u - 1) * per + k + 1)

        def unit(j):
            sbk, t = UNITS[j // 2]
            return j % 2, sbk, t, max(0, P * t - BLK * sbk)

        def pe_item(pe, u, b, n, h, first):
            wait_bank(pe, u, n, first)
            dst = pbank(n)
            kind, k, _ = ITEMS[n]
            if kind == "qk":
                if k == 0 and b == 0:
                    pe.wait_ge(s_wq, 8 * u + 16)
                w = wqkv[:, (k % 2) * D:(k % 2 + 1) * D]
                c = b * SEQ + (k // 2) * BLK
                pe.matmul(dst, w, xT[:, c:c + BLK], start=True, stop=True).then_inc(s_prep_qk, 1)
            elif kind == "v":
                for t in range(4):
                    c = b * SEQ + (4 * k + t) * P
                    mm = pe.matmul(dst[:, t * P:(t + 1) * P], xT[:, c:c + P], wqkv[:, 2 * D:3 * D], start=True, stop=True)
                mm.then_inc(s_prep_v, 1)
            elif kind == "max":
                h, s, c, w = PIECES[k]
                if k in (0, NPIECE0):
                    pe.wait_ge(s_qk_lo, u * 8 + (4 if k == 0 else 8))
                diag = c + w == P * (s + 1)
                mm = pe.matmul(dst[:, 0:w], qa[:, b, h, s * P:(s + 1) * P], ka[:, b, h, c:c + w], start=True, stop=not diag)
                if diag:
                    mm = pe.matmul(dst[:, w - P:w], idb[:, :], msb[:, :], start=False, stop=True)
                mm.then_inc(s_prep_m, 1)
            else:
                pe.wait_ge(s_mneg, 2 * u + 2)
                pe.transpose(dst[0:MROWS, 0:P], mx[:, :, :].rearrange("p h s -> p (h s)"), ident).then_inc(s_prep_t, 1)

        def act_item(act, u, b, n, h, first):
            src = pbank(n)
            kind, k, _ = ITEMS[n]
            if kind == "qk":
                c = slice((k // 2) * BLK, (k // 2 + 1) * BLK)
                bias = wqkv[h * DH:(h + 1) * DH, 3 * D + k % 2:3 * D + k % 2 + 1]
                if h == 0:
                    act.wait_ge(s_prep_qk, 4 * u + k + 1)
                if k % 2 == 0:
                    outs = [qa[0:DH, b, h, c], qa[DH:P, b, h, c]]
                else:
                    outs = [ka[0:DH, b, h, c], kb[0:DH, b, h, c]] + ([ka[DH:P, b, h, c]] if h == 1 else [])
                for o in outs:
                    i = act.activation(o, src[h * DH:(h + 1) * DH, :], ACT.Identity, bias=bias)
                i.then_inc(s_qk_hi, 1)
            elif kind == "v" and h == 0:
                act.wait_ge(s_prep_v, 2 * u + k + 1)
                act.activation(v[:, b, 4 * k:4 * k + 4, :].rearrange("p t d -> p (t d)"), src, ACT.Copy).then_inc(s_v, 1)

        def dve_item(dve, u, b, n, h, first):
            src = pbank(n)
            kind, k, _ = ITEMS[n]
            if kind == "qk":
                c = slice((k // 2) * BLK, (k // 2 + 1) * BLK)
                hp = slice(h * DH, (h + 1) * DH)
                bias = wqkv[hp, 3 * D + k % 2:3 * D + k % 2 + 1]
                dve.wait_ge(s_qk_hi, 8 * u + 2 * k + h + 1)
                if k % 2 == 0:
                    o, hi = qb[0:DH, b, h, c], qa[hp, b, h, c]
                else:
                    o, hi = ka[DH:P, b, h, c], ka[hp, b, h, c]
                dve.scalar_tensor_tensor(out=o, in0=src[hp, :], scalar=bias, in1=hi, op0=ALU.add, op1=ALU.subtract).then_inc(s_qk_lo, 1)
            elif kind == "max":
                h, s, c, w = PIECES[k]
                dve.wait_ge(s_prep_m, NPIECE * u + k + 1)
                if k == 0 and not first:
                    dve.wait_ge(s_prep_t, u)
                o = mx[:, h, s:s + 1] if c == 0 else mx2[:, h, s - TB // 2:s - TB // 2 + 1]
                dve.tensor_reduce(o, src[:, 0:w], AX.X, ALU.max).then_inc(s_pmax, 1)
                if k == NPIECE - 1:
                    dve.wait_ge(s_pmax, NPIECE * (u + 1))
                    dve.tensor_tensor(mx[:, :, TB // 2:TB], mx[:, :, TB // 2:TB], mx2[:, :, :], ALU.max).then_inc(s_mneg, 1)
                    dve.wait_ge(s_mneg, 2 * u + 1)
                    dve.tensor_scalar(mx[:, :, :], mx[:, :, :], -1.0, None, ALU.mult).then_inc(s_mneg, 1)
            elif kind == "turn":
                dve.wait_ge(s_prep_t, u + 1)
                for h in range(2):
                    o = qb[DH:KB_ROWS, b, h, :].rearrange("r (s c) -> r s c", s=TB)
                    src3 = src[0:MROWS, 0:P].rearrange("r (o c) -> r o c", o=1).to_broadcast([MROWS, TB, P])
                    dve.tensor_tensor(o, src3, mD[:, h, :, :], ALU.mult).then_inc(s_mrow, 1)

        def pe_scores(pe, u, b, j, first):
            h, sbk, t, o = unit(j)
            w = BLK - o
            if j == 0:
                pe.wait_ge(s_mrow, 2 * u + 2)
                pe.wait_ge(s_v, 2 * u + 2)
                if first:
                    pe.wait_ge(s_cbe, 5)
            if j % 2 and j >= 3:
                pe.wait_ge(s_exp, NU * u + j - 2)
            dst = banks[:, j % 3, 0:w]
            q = slice(sbk * BLK + o, (sbk + 1) * BLK)
            k = slice(t * P, (t + 1) * P)
            diag = P * t >= BLK * sbk
            pe.matmul(dst, ka[:, b, h, k], qa[:, b, h, q], start=True, stop=False)
            mm = pe.matmul(dst, kb[0:KB_ROWS, b, h, k], qb[0:KB_ROWS, b, h, q], start=False, stop=not diag)
            if diag:
                mm = pe.matmul(dst[:, 0:P], idb[:, :], mtb[:, :], start=False, stop=True)
            mm.then_inc(s_st, 1)

        def pe_pv(pe, u, b, j, first):
            h, sbk, t, o = unit(j)
            pe.wait_ge(s_exp, NU * u + j + 1)
            if t == 0 and h == 0 and not first:
                pe.wait_ge(s_zz, 2 * u + sbk - 1)
            pe.matmul(banks[h * DH:(h + 1) * DH, 4 + sbk, o:BLK], v[:, b, t, h * DH:(h + 1) * DH],
                      pr[:, j % NP0, 0:BLK - o], start=(t == 0),
                      stop=(t == (sbk + 1) * TB // 2 - 1)).then_inc(s_pv, 1)

        def pe_tail(pe, u, sbk, stage, first):
            n = 2 * u + sbk
            if stage == 0:
                pe.wait_ge(s_padd, NU * u + (SB0_UNITS if sbk == 0 else NU))
                if sbk == 1:
                    pe.wait_ge(s_zz, n)
                elif not first:
                    pe.wait_ge(s_xacc, u)
                for i in range(2 * NCH):
                    h, c = divmod(i, NCH)
                    mm = pe.matmul(banks[:, 6, 2 * i:2 * i + 2], pacc[:, sbk, h, c * P:(c + 1) * P], ones[:, :], start=True, stop=True)
                mm.then_inc(s_sum, 1)
            elif stage == 1:
                pe.wait_ge(s_rcp, 3 * n + 3)
                pe.transpose(banks[0:RROWS, 6, P:2 * P], rcp[:, 0:2, :].bitcast(F32).rearrange("p k i -> p (k i)"), ident).then_inc(s_rt, 1)
            else:
                pe.wait_ge(s_rex, n + 1)
                pe.matmul(banks[:, 6, :], spr[:, :], rex.rearrange("r c q -> r (c q)"), start=True, stop=True).then_inc(s_spread, 1)

        def pe_out(pe, u, b, p):
            pe.wait_ge(s_zz, 2 * u + 2)
            for i in range(TB):
                for h in range(2):
                    mm = pe.matmul(banks[h * DH:(h + 1) * DH, 6, 0:D], zz[:, h, i:SEQ // 2:TB], wpr[:, i, :],
                                   start=(i == 0), stop=(i == TB - 1))
            mm.then_inc(s_op, 1)

        def act_tail(act, u, sbk, stage, first):
            if stage == 2:
                n = 2 * u + sbk
                act.wait_ge(s_spread, n + 1)
                if not (first and sbk == 0):
                    act.wait_ge(s_zz, n)
                act.activation(rall[:, :], banks[:, 6, :], ACT.Copy).then_inc(s_rall, 1)

        def dve_tail(dve, u, sbk, stage, first):
            n = 2 * u + sbk
            if stage == 0:
                whole, hi, lo = rcp[:, 2, :].bitcast(F32), rcp[:, 0, :], rcp[:, 1, :]
                dve.wait_ge(s_sum, n + 1)
                dve.reciprocal(whole, banks[:, 6, 0:4 * NCH:2]).then_inc(s_rcp, 1)
                dve.wait_ge(s_rcp, 3 * n + 1)
                dve.tensor_copy(hi, whole).then_inc(s_rcp, 1)
                dve.wait_ge(s_rcp, 3 * n + 2)
                dve.tensor_tensor(lo, whole, hi, ALU.subtract).then_inc(s_rcp, 1)
            elif stage == 1:
                dve.wait_ge(s_rt, n + 1)
                dve.tensor_tensor(rex, banks[0:RROWS, 6, P:2 * P].rearrange("r (o q) -> r o q", o=1).to_broadcast([RROWS, NCH, P]),
                                  mR[:, :, :], ALU.mult).then_inc(s_rex, 1)
            else:
                dve.wait_ge(s_rall, n + 1)
                dve.wait_ge(s_pv, NU * u + (SB0_UNITS if sbk == 0 else NU))
                if sbk == 0 and not first:
                    dve.wait_ge(s_op, u)
                half = BLK // 2
                for h in range(2):
                    hp = slice(h * DH, (h + 1) * DH)
                    for odd in range(2):
                        i = dve.tensor_tensor(zz[odd * DH:(odd + 1) * DH, h, sbk * half:(sbk + 1) * half],
                                              banks[hp, 4 + sbk, odd:BLK:2], rall[hp, odd:BLK:2], ALU.mult)
                i.then_inc(s_zz, 1)

        def dve_acc(dve, u, b, p):
            dve.wait_ge(s_op, u + 1)
            xs = x[:, b * TB + p, :] if isinstance(p, int) else x[:, bass.ds(b * TB + p, 1), :].rearrange("p o d -> p (o d)")
            dve.scalar_tensor_tensor(out=xs, in0=banks[:, 6, 0:D], scalar=SCALE0, in1=xs, op0=ALU.mult, op1=ALU.add).then_inc(s_xacc, 1)

        def attention0(e, work, end, item, slot, tail, tail_out, rest):
            for j in sorted(work):
                for n, h in work[j]:
                    item(e, 0, 0, n, h, True)

            def pair(p, first, last):
                for b in range(BATCH):
                    u = 2 * p + b
                    f, l = first and b == 0, last and b == 1
                    for j in range(NU):
                        slot(e, u, b, j, f)
                        if not l:
                            for n, h in work.get(j, ()):
                                item(e, u + 1, 1 - b, n, h, False)
                        for back, sbk, stage in end.get(j, ()):
                            if stage == 3 and not f:
                                tail_out(e, u - 1, 1 - b, p - 1 + b)
                            elif stage < 3 and not (back and f):
                                tail(e, u - back, sbk, stage, f)
                        rest(e, u, b, j, f)
            pair(0, True, False)
            with e.Fori(1, PAIRS - 1) as p:
                pair(p, False, False)
            pair(PAIRS - 1, False, True)
            for stage in range(3):
                tail(e, 2 * PAIRS - 1, 1, stage, False)
            tail_out(e, 2 * PAIRS - 1, 1, PAIRS - 1)

        def linear_pe(pe):
            pe.wait_ge(s_fw, 64)
            pe.wait_ge(ln[1]["xT"], 4)
            for n in range(NT):
                mm = pe.matmul(banks[:, 4 + n // TB, (n % TB) * DOWN:(n % TB + 1) * DOWN], xT[:, n * P:(n + 1) * P], wdn[:, :],
                               start=True, stop=True)
                if n % TB == TB - 1:
                    mm.then_inc(s_dn, 1)
            pe.wait_ge(s_ch, 24)
            for n in range(NT):
                mm = pe.transpose(banks[0:RSUM + 1, (6, 7, 4, 5)[n // 4], (n % 4) * P:(n % 4 + 1) * P], hg[:, n, :], ident)
                if n % 4 == 3:
                    mm.then_inc(s_hT, 1)
            for n in range(NT):
                if n % 4 == 0:
                    pe.wait_ge(s_hTe, n // 4 + 1)
                o = banks[:, n // 4, (n % 4) * P:(n % 4 + 1) * P]
                pe.matmul(o, xT[:, n * P:(n + 1) * P], wbase[:, :], start=True, stop=False)
                mm = pe.matmul(o, hgT[:, n * P:(n + 1) * P], wup[:, :], start=False, stop=True)
                if n % 4 == 3:
                    mm.then_inc(s_fo, 1)

        def linear_act(act):
            for i in range(2):
                act.wait_ge(s_dn, i + 1)
                act.activation(dn[:, i * TB:(i + 1) * TB, :].rearrange("p n c -> p (n c)"), banks[:, 4 + i, 0:TB * DOWN], ACT.Copy)\
                   .then_inc(s_dne, 1)
            act.wait_ge(s_ch, 5)
            act.activation(nrm[:, :], nrm[:, :], ACT.Sqrt).then_inc(s_fa, 1)
            act.wait_ge(s_ch, 6)
            act.activation(escale[:, :], escale[:, :], ACT.Exp).then_inc(s_fa, 1)
            act.wait_ge(s_ch, 15)
            act.activation(lg[:, :, :], lg[:, :, :], ACT.Exp).then_inc(s_fa, 1)
            for i in range(4):
                act.wait_ge(s_hT, i + 1)
                act.activation(hgT[:, i * BLK:(i + 1) * BLK], banks[0:RSUM + 1, (6, 7, 4, 5)[i], :], ACT.Copy).then_inc(s_hTe, 1)

        def linear_dve(dve):
            done = [0]

            def step(ins, wait=True):
                ins.then_inc(s_ch, 1)
                done[0] += 1
                if wait:
                    dve.wait_ge(s_ch, done[0])

            def wide(t, n):
                return t.rearrange("p (n o) -> p n o", o=1).to_broadcast([P, t.shape[1], n])
            sim = small[:, PROJ:PROJ + NE0 * PROJ].rearrange("p (e k) -> p e k", e=NE0)
            dve.wait_ge(s_fw, 64)
            dve.wait_ge(s_dne, 2)
            step(dve.tensor_tensor(pj[:, :, :], dn[:, :, 0:PROJ],
                                   small[:, 0:PROJ].rearrange("p (o k) -> p o k", o=1).to_broadcast([P, NT, PROJ]), ALU.add))
            step(dve.tensor_tensor(sq[:, :, :], pj[:, :, :], pj[:, :, :], ALU.mult))
            step(dve.tensor_tensor(simq[:, :, :], sim, sim, ALU.mult))
            step(dve.tensor_reduce(nrm[:, 0:NT], sq[:, :, :], AX.X, ALU.add), False)
            step(dve.tensor_reduce(nrm[:, NT:NT + NE0], simq[:, :, :], AX.X, ALU.add), False)
            step(dve.tensor_scalar(escale[:, :], small[:, PROJ + NE0 * PROJ:], CLAMP, None, ALU.min), False)
            dve.wait_ge(ln[1]["turned"], 4)
            step(dve.tensor_tensor(prod, pj[:, :, :].rearrange("p n (o k) -> p n o k", o=1).to_broadcast([P, NT, NE0, PROJ]),
                                   sim.rearrange("p (o e) k -> p o e k", o=1).to_broadcast([P, NT, NE0, PROJ]), ALU.mult))
            step(dve.tensor_reduce(lw[:, :, :], prod, AX.X, ALU.add), False)
            dve.wait_ge(s_fa, 1)
            step(dve.tensor_scalar(nrm[:, :], nrm[:, :], 1e-12, None, ALU.max))
            step(dve.reciprocal(nrm[:, :], nrm[:, :]))
            dve.wait_ge(s_fa, 2)
            step(dve.tensor_scalar(nrm[:, NT:], nrm[:, NT:], escale[:, 0:1], None, ALU.mult))
            step(dve.tensor_tensor(lw[:, :, :], lw[:, :, :], wide(nrm[:, 0:NT], NE0), ALU.mult))
            step(dve.tensor_tensor(lw[:, :, :], lw[:, :, :],
                                   nrm[:, NT:].rearrange("p (o e) -> p o e", o=1).to_broadcast([P, NT, NE0]), ALU.mult))
            step(dve.tensor_reduce(col[:, 0, :], lw[:, :, :], AX.X, ALU.max))
            step(dve.tensor_tensor(lg[:, :, :], lw[:, :, :], wide(col[:, 0, :], NE0), ALU.subtract))
            dve.wait_ge(s_fa, 3)
            step(dve.tensor_reduce(col[:, 1, :], lg[:, :, :], AX.X, ALU.add))
            step(dve.reciprocal(col[:, 1, :], col[:, 1, :]))
            step(dve.tensor_tensor(lg[:, :, :], lg[:, :, :], wide(col[:, 1, :], NE0), ALU.mult))
            step(dve.tensor_reduce(col[:, 2, :], lg[:, :, :], AX.X, ALU.max))
            step(dve.tensor_tensor(lw[:, :, :], lg[:, :, :], wide(col[:, 2, :], NE0), ALU.is_equal))
            step(dve.tensor_tensor(lw[:, :, :], lw[:, :, :],
                                   cst[:, C_FIRST:C_FIRST + NE0].rearrange("p (o e) -> p o e", o=1).to_broadcast([P, NT, NE0]),
                                   ALU.mult))
            step(dve.tensor_reduce(col[:, 3, :], lw[:, :, :], AX.X, ALU.max))
            dve.tensor_tensor(lw[:, :, :], lw[:, :, :], wide(col[:, 3, :], NE0), ALU.is_equal).then_inc(s_dne, 1)
            dve.wait_ge(s_dne, 3)
            step(dve.tensor_tensor(lw[:, :, :], lw[:, :, :], lg[:, :, :], ALU.mult))
            r0 = 0
            for e, r in enumerate(RANKS):
                i = dve.tensor_tensor(hg[:, :, r0:r0 + r], dn[:, :, PROJ + r0:PROJ + r0 + r],
                                      lw[:, :, e:e + 1].to_broadcast([P, NT, r]), ALU.mult)
                r0 += r
            step(i, False)
            for i in range(4):
                dve.wait_ge(s_fo, i + 1)
                xs = x[:, 4 * i:4 * i + 4, :].rearrange("p t d -> p (t d)")
                dve.tensor_tensor(xs, banks[:, i, :], xs, ALU.add).then_inc(s_fx, 1)

        PJ_AT, HI_AT = 16, 21
        SUM_AT, OUT_AT = 1, 11

        def setup1_pe(pe):
            pe.wait_ge(s_aw, 48)
            pe.wait_ge(ln[2]["xT"], 4)
            pe.matmul(banks[:, 4, 0:P], wvT[:, :], wkT[:, :], start=True, stop=True).then_inc(s_a1, 1)
            for n in range(NT):
                mm = pe.matmul(banks[:, n // 4, (n % 4) * P:(n % 4 + 1) * P], xT[:, n * P:(n + 1) * P], wkT[:, :], start=True, stop=True)
                if n % 4 == 3:
                    mm.then_inc(s_qt, 1)
            pe.wait_ge(s_a1m, 2)
            for g in range(GROUPS):
                mm = pe.matmul(banks[:, 5, g * P:(g + 1) * P], a1[:, g, :, :].rearrange("p h j -> p (h j)"), woT[:, :], start=True, stop=True)
            mm.then_inc(s_gg, 1)
            pe.wait_ge(s_gge, 1)
            pe.wait_ge(s_qte, 4)

        def setup1_act(act):
            for i in range(4):
                act.wait_ge(s_qt, i + 1)
                act.activation(qtm[:, 4 * i:4 * i + 4, :].rearrange("p t d -> p (t d)"), banks[:, i, :], ACT.Copy).then_inc(s_qte, 1)
            act.wait_ge(s_gg, 1)
            act.activation(gg[:, :, :].rearrange("p g d -> p (g d)"), banks[:, 5, :], ACT.Copy).then_inc(s_gge, 1)

        def setup1_dve(dve):
            dve.memset(a1[:, :, :, :].rearrange("p g h j -> p (g h j)"), 0.0).then_inc(s_a1m, 1)
            dve.memset(qv[:, :, :, :, :].rearrange("p b t h j -> p (b t h j)"), 0.0).then_inc(s_qv, 1)
            dve.wait_ge(s_qv, 1)
            dve.memset(qv[:, :, :, :, DK:DK + 1].rearrange("p b t h j -> p (b t h) j"), 1.0).then_inc(s_qv, 1)
            dve.wait_ge(s_a1m, 1)
            dve.wait_ge(s_a1, 1)
            bd = cst[:, C_BD:C_BD + P]
            dve.scalar_tensor_tensor(out=a1[:, :, :, 0:DK].rearrange("p g h j -> p (g h) j"),
                                     in0=banks[:, 4, 0:P].rearrange("p (h j) -> p h j", j=DK), scalar=SCALE1,
                                     in1=bd.rearrange("p (h j) -> p h j", j=DK), op0=ALU.mult, op1=ALU.mult).then_inc(s_a1m, 1)
            dve.wait_ge(s_qv, 2)
            dve.wait_ge(s_qte, 4)

        def prep1_pe(pe, u, b, g, first, part):
            if part == 0:
                pe.wait_ge(s_wk, 8 * (u - b) + 16)
                if not first:
                    pe.wait_ge(s_x1, 2 * (u - 1))
                for hf in range(2):
                    pe.matmul(banks[0:96, 6 + hf, :], wk3[:, :], xT[:, b * SEQ + hf * BLK:b * SEQ + (hf + 1) * BLK],
                              start=True, stop=True).then_inc(s_pj, 1)
            else:
                for hf in range(2):
                    pe.wait_ge(s_sq, 2 * u + hf + 1)
                    pe.matmul(banks[96:P, 6 + hf, :], cst[0:96, C_BLK:C_BLK + 32], sq1[:, hf * BLK:(hf + 1) * BLK],
                              start=True, stop=True).then_inc(s_nm, 1)

        def prep1_act(act, u, b, g, first, part):
            for hf in range(2):
                c = slice(hf * BLK, (hf + 1) * BLK)
                if part == 0:
                    act.wait_ge(s_pj, 2 * u + hf + 1)
                    act.activation(sq1[:, c], banks[0:96, 6 + hf, :], ACT.Square).then_inc(s_sq, 1)
                else:
                    act.wait_ge(s_nm, 2 * u + hf + 1)
                    act.activation(hi1[:, b, c], banks[:, 6 + hf, :], ACT.Copy).then_inc(s_hi, 1)

        def prep1_dve(dve, u, b, g, first, part):
            if part == 0:
                gs = g * GH * DK
                src = (qtm[:, b * TB:(b + 1) * TB, gs:gs + GH * DK] if isinstance(g, int) else
                       qtm[:, b * TB:(b + 1) * TB, bass.ds(gs, GH * DK)])
                if not isinstance(u, int) or u >= 2:
                    dve.wait_ge(s_pv1, 2 * TB * (u - 1))
                dve.tensor_scalar(qv[:, b, :, :, 0:DK], src.rearrange("p t (h k) -> p t h k", k=DK), 1.0, None, ALU.mult).then_inc(s_qv, 1)
                return
            cc = cst[:, C_COL:C_COL + 6]
            for hf in range(2):
                c = slice(hf * BLK, (hf + 1) * BLK)
                dve.wait_ge(s_hi, 2 * u + hf + 1)
                for k, t in enumerate((r1, l1)):
                    dve.tensor_scalar(t[:, b, c], hi1[:, b, c], cc[:, 3 * k + 1:3 * k + 2], cc[:, 3 * k + 2:3 * k + 3], ALU.mult, ALU.add)\
                       .then_inc(s_rl, 1)
                for k, t in enumerate((r1, l1)):
                    dve.wait_ge(s_rl, 8 * u + 4 * hf + k + 1)
                    dve.scalar_tensor_tensor(out=t[:, b, c], in0=banks[:, 6 + hf, :], scalar=cc[:, 3 * k:3 * k + 1], in1=t[:, b, c],
                                             op0=ALU.mult, op1=ALU.add).then_inc(s_rl, 1)
            dve.wait_ge(s_rl, 8 * u + 8)
            for h in range(GH):
                dve.tensor_scalar(l1h(b, h), l1[:, b, :], cst[:, C_MASK + h:C_MASK + h + 1], None, ALU.mult).then_inc(s_lh, 1)

        def slot1_pe(pe, u, b, j, first):
            t, h = divmod(j, GH)
            if j == 0:
                pe.wait_ge(s_lh, GH * (u + 1))
                pe.wait_ge(s_qv, u + 3)
            if not (first and j < 2):
                pe.wait_ge(s_exp1, NSLOT * u + j - 1)
            for sbk in range(2):
                mm = pe.matmul(banks[:, 2 * (j % 2) + sbk, :], l1h(b, h)[:, t * P:(t + 1) * P], r1[:, b, sbk * BLK:(sbk + 1) * BLK],
                               start=True, stop=True)
            mm.then_inc(s_st1, 1)
            if j % 2 and t > 0:
                pv1(pe, u, b, t - 1, h // 2, first)
            if j == NSLOT - 1:
                pv1(pe, u, b, t, 0, first)
                pv1(pe, u, b, t, 1, first)

        def pv1(pe, u, b, t, sbk, first):
            pe.wait_ge(s_exp1, NSLOT * u + GH * (t + 1))
            if t == 0 and not first:
                pe.wait_ge(s_zs, 2 * (u - 1) + sbk + 1)
            for h in range(GH):
                mm = pe.matmul(banks[32 * h:32 * h + 32, 4 + sbk, :], qv[:, b, t, h, :], pr[:, (GH * t + h) % NP1, sbk * BLK:(sbk + 1) * BLK],
                               start=(t == 0), stop=(t == TB - 1))
            mm.then_inc(s_pv1, 1)

        def slot1_act(act, u, b, j, first):
            t = j // GH
            act.wait_ge(s_st1, NSLOT * u + j + 1)
            if not (first and t < 2):
                act.wait_ge(s_pv1, 2 * TB * u + 2 * (t - 1))
            act.activation(pr[:, j % NP1, :], banks[:, 2 * (j % 2):2 * (j % 2) + 2, :].rearrange("p b c -> p (b c)"), ACT.Exp,
                           scale=2 * SCALE1).then_inc(s_exp1, 1)

        def sums1_pe(pe, u, b, g):
            for hf in range(2):
                pe.wait_ge(s_zs, 2 * u + hf + 1)
                if hf == 0:
                    pe.wait_ge(s_lh, GH * (u + 1))
                pe.matmul(banks[:, 6 + hf, :], cst[:, C_SEL:C_SEL + P], zs[:, hf * BLK:(hf + 1) * BLK], start=True, stop=True).then_inc(s_sum1, 1)

        def sums1_dve(dve, u, b, g):
            for hf in range(2):
                c = slice(hf * BLK, (hf + 1) * BLK)
                dve.wait_ge(s_pv1, 2 * TB * u + 2 * TB - 1 + hf)
                if not isinstance(u, int) or u > 0:
                    dve.wait_ge(s_zn, 2 * u)
                dve.tensor_copy(zs[:, c], banks[:, 4 + hf, :]).then_inc(s_zs, 1)
            for hf in range(2):
                c = slice(hf * BLK, (hf + 1) * BLK)
                dve.wait_ge(s_sum1, 2 * u + hf + 1)
                dve.reciprocal(rz[:, c], banks[:, 6 + hf, :]).then_inc(s_rz, 1)
                dve.wait_ge(s_rz, 2 * u + hf + 1)
                if not isinstance(u, int) or u > 0:
                    dve.wait_ge(s_op1, 2 * u)
                dve.tensor_tensor(zn[:, c], zs[:, c], rz[:, c], ALU.mult).then_inc(s_zn, 1)

        def out1_pe(pe, u, b, g):
            w = gg[:, g, :] if isinstance(g, int) else gg[:, bass.ds(g, 1), :].rearrange("p o d -> p (o d)")
            for hf in range(2):
                pe.wait_ge(s_zn, 2 * u + hf + 1)
                for t in range(4):
                    c = hf * BLK + t * P
                    mm = pe.matmul(banks[:, 6 + hf, t * P:(t + 1) * P], zn[:, c:c + P], w, start=True, stop=True)
                mm.then_inc(s_op1, 1)

        def out1_dve(dve, u, b, g):
            for hf in range(2):
                dve.wait_ge(s_op1, 2 * u + hf + 1)
                xs = x[:, b * TB + 4 * hf:b * TB + 4 * hf + 4, :].rearrange("p t d -> p (t d)")
                dve.tensor_tensor(xs, banks[:, 6 + hf, :], xs, ALU.add).then_inc(s_x1, 1)

        def attention1(e, prep, slot, sums, outp):
            prep(e, 0, 0, 0, True, 0)
            prep(e, 0, 0, 0, True, 1)

            def group(g, first, last):
                for b in range(BATCH):
                    u = 2 * g + b
                    f, l = first and b == 0, last and b == 1
                    for j in range(NSLOT):
                        slot(e, u, b, j, f)
                        if not l and j in (PJ_AT, HI_AT):
                            prep(e, u + 1, 1 - b, g + b, False, int(j == HI_AT))
                        if not f and j == SUM_AT:
                            sums(e, u - 1, 1 - b, g - 1 + b)
                        if not f and j == OUT_AT:
                            outp(e, u - 1, 1 - b, g - 1 + b)
            group(0, True, False)
            with e.Fori(1, GROUPS - 1) as g:
                group(g, False, False)
            group(GROUPS - 1, False, True)
            sums(e, 2 * GROUPS - 1, 1, GROUPS - 1)
            outp(e, 2 * GROUPS - 1, 1, GROUPS - 1)

        def gates_pe(pe):
            pe.wait_ge(s_mw, 48)
            pe.wait_ge(ln[3]["xT"], 4)
            for i in range(4):
                pe.matmul(banks[0:RH, i, :], wr[:, 0:RH], xT[:, i * BLK:(i + 1) * BLK], start=True, stop=True).then_inc(s_rh, 1)
            pe.wait_ge(s_rhe, 5)
            for n in range(NT):
                mm = pe.matmul(banks[:, 4, n * NE1:(n + 1) * NE1], rT[:, n * P:(n + 1) * P], wr2[:, :], start=True, stop=True)
            mm.then_inc(s_lo, 1)

        def gates_act(act):
            for i in range(4):
                act.wait_ge(s_rh, i + 1)
                act.activation(rT[0:RH, i * BLK:(i + 1) * BLK], banks[0:RH, i, :], ACT.Relu, bias=wr[0:RH, RH:RH + 1]).then_inc(s_rhe, 1)
            act.wait_ge(s_gc, 2)
            act.activation(ga[:, :, :], gl[:, :, :], ACT.Exp).then_inc(s_ga, 1)
            act.wait_ge(s_gc, 11)
            act.activation(col[:, 2, :], col[:, 2, :], ACT.Exp, scale=0.5).then_inc(s_ga, 1)

        def gates_dve(dve):
            done = [0]
            for i in range(4):
                c = slice(i * BLK, (i + 1) * BLK)
                dve.wait_ge(ln[3]["xT"], i + 1)
                dve.tensor_copy(x2[:, 0, c], xT[:, c]).then_inc(s_xs, 1)
                dve.wait_ge(s_xs, 2 * i + 1)
                dve.tensor_tensor(x2[:, 1, c], xT[:, c], x2[:, 0, c], ALU.subtract).then_inc(s_xs, 1)

            def step(ins):
                ins.then_inc(s_gc, 1)
                done[0] += 1
                dve.wait_ge(s_gc, done[0])

            def wide(t):
                return t.rearrange("p (n o) -> p n o", o=1).to_broadcast([P, NT, NE1])
            marks = cst[:, C_FIRST:C_FIRST + NE1].rearrange("p (o e) -> p o e", o=1).to_broadcast([P, NT, NE1])
            dve.memset(gw[:, :, 0:1].rearrange("p n o -> p (n o)"), 1.0).then_inc(s_gTe, 1)
            dve.memset(onesr[:, :].bitcast(F32), 1.0).then_inc(s_gTe, 1)
            dve.memset(gsel[:, :, :].bitcast(F32).rearrange("p k c -> p (k c)"), 0.0).then_inc(s_gTe, 1)
            dve.wait_ge(s_gTe, 3)
            dve.wait_ge(s_lo, 1)
            lo = banks[:, 4, 0:NT * NE1].rearrange("p (n e) -> p n e", e=NE1)
            step(dve.tensor_reduce(col[:, 0, :], lo, AX.X, ALU.max))
            step(dve.tensor_tensor(gl[:, :, :], lo, wide(col[:, 0, :]), ALU.subtract))
            dve.wait_ge(s_ga, 1)
            step(dve.tensor_reduce(col[:, 1, :], ga[:, :, :], AX.X, ALU.add))
            step(dve.reciprocal(col[:, 1, :], col[:, 1, :]))
            step(dve.tensor_tensor(ga[:, :, :], ga[:, :, :], wide(col[:, 1, :]), ALU.mult))
            step(dve.tensor_reduce(col[:, 0, :], ga[:, :, :], AX.X, ALU.max))
            for k, oh in enumerate((oh1, oh2)):
                g = ga[:, :, :] if k == 0 else gl[:, :, :]
                m = col[:, 2 * k, :]
                dve.tensor_tensor(oh[:, :, :], g, wide(m), ALU.is_equal).then_inc(s_b2, 1)
                dve.wait_ge(s_b2, 3 * k + 1)
                dve.tensor_tensor(oh[:, :, :], oh[:, :, :], marks, ALU.mult).then_inc(s_b2, 1)
                dve.wait_ge(s_b2, 3 * k + 2)
                dve.tensor_reduce(col[:, 3, :], oh[:, :, :], AX.X, ALU.max).then_inc(s_b2, 1)
                dve.wait_ge(s_b2, 3 * k + 3)
                step(dve.tensor_tensor(oh[:, :, :], oh[:, :, :], wide(col[:, 3, :]), ALU.is_equal))
                if k == 0:
                    step(dve.scalar_tensor_tensor(out=gl[:, :, :], in0=oh[:, :, :], scalar=-4.0, in1=ga[:, :, :],
                                                  op0=ALU.mult, op1=ALU.add))
                    step(dve.tensor_reduce(col[:, 2, :], gl[:, :, :], AX.X, ALU.max))
            step(dve.tensor_tensor(col[:, 2, :], col[:, 2, :], col[:, 0, :], ALU.subtract))
            dve.wait_ge(s_ga, 2)
            step(dve.tensor_scalar(col[:, 1, :], col[:, 2, :], 1.0, None, ALU.add))
            step(dve.reciprocal(col[:, 1, :], col[:, 1, :]))
            step(dve.tensor_tensor(col[:, 2, :], col[:, 2, :], col[:, 1, :], ALU.mult))
            step(dve.tensor_tensor(oh1[:, :, :], oh1[:, :, :], wide(col[:, 1, :]), ALU.mult))
            step(dve.tensor_tensor(oh2[:, :, :], oh2[:, :, :], wide(col[:, 2, :]), ALU.mult))
            step(dve.tensor_tensor(gw[:, :, 1:], oh1[:, :, :], oh2[:, :, :], ALU.add))
            hi, lo = gw2[:, :, 0, :], gw2[:, :, 1, :]
            step(dve.tensor_copy(hi, gw[:, :, :]))
            step(dve.tensor_tensor(lo, gw[:, :, :], hi, ALU.subtract))
            for i in range(4):
                dve.wait_ge(s_gT, i + 1)
                dve.tensor_copy(gT[:, i * BLK:(i + 1) * BLK], banks[0:GROWS, i, :]).then_inc(s_gTe, 1)
            dve.wait_ge(s_gTe, 7)
            split_dve(dve, 0, 0, True)

        def bias_pe(pe):
            pe.wait_ge(s_gc, 19)
            for i in range(4):
                for t in range(4):
                    mm = pe.transpose(banks[0:GROWS, i, t * P:(t + 1) * P], gw2[:, 4 * i + t, :, :].bitcast(F32).rearrange("p k e -> p (k e)"), ident)
                mm.then_inc(s_gT, 1)
            for i in range(4):
                pe.wait_ge(s_gTe, 4 + i)
                pe.matmul(banks[:, 4 + i, :], b2[:, :], gT[:, i * BLK:(i + 1) * BLK], start=True, stop=False)
            pe.wait_ge(s_gTe, 7)

        def split_dve(dve, q, w, first):
            dve.wait_ge(s_ew[w], 8 * (q - w) + 16)
            if not first:
                dve.wait_ge(s_down, 4 * (q - 1))
            dve.tensor_copy(w2[:, w, 0, :], w1[:, w, 0:2 * INNER]).then_inc(s_ws, 1)
            dve.wait_ge(s_ws, 2 * q + 1)
            dve.tensor_tensor(w2[:, w, 1, :], w1[:, w, 0:2 * INNER], w2[:, w, 0, :], ALU.subtract).then_inc(s_ws, 1)

        def select_dve(dve, q, tb, first):
            k = 4 * q + tb
            if not (first and tb < 2):
                dve.wait_ge(s_spreadg, k - 1)
            c = cst[0:GROWS, C_EXP + q:C_EXP + q + 1] if isinstance(q, int) else cst[0:GROWS, bass.ds(q + C_EXP, 1)]
            dve.tensor_scalar(gsel[:, tb % 2, :], gT[:, tb * BLK:(tb + 1) * BLK], c, None, ALU.mult).then_inc(s_gs, 1)

        def up_pe(pe, q, w, tb, first):
            k = 4 * q + tb
            if tb == 0:
                pe.wait_ge(s_ws, 2 * q + 2)
            if first:
                pe.wait_ge(s_xs, 2 * tb + 2)
            if not (first and tb == 0):
                pe.wait_ge(s_hid, NI * k)
            c = slice(tb * BLK, (tb + 1) * BLK)
            for i in range(NI):
                if i == 3:
                    pe.wait_ge(s_hid, NI * k + 1)
                for j, (a_, b_) in enumerate(((0, 0), (0, 1), (1, 0))):
                    mm = pe.matmul(banks[:, i % 3, :], w2[:, w, a_, i * P:(i + 1) * P], x2[:, b_, c], start=(j == 0), stop=(j == 2))
                mm.then_inc(s_up, 1)
                if i == 0:
                    pe.wait_ge(s_gs, k + 1)
                    if not (first and tb == 0):
                        pe.wait_ge(s_gh, NI * k)
                    pe.matmul(banks[:, 3, :], onesr[:, :], gsel[:, tb % 2, :], start=True, stop=True).then_inc(s_spreadg, 1)

        def down_pe(pe, q, w, tb, first):
            k = 4 * q + tb
            last = isinstance(q, int) and q == NE1
            for i in range(NI):
                pe.wait_ge(s_hl, NI * k + i + 1)
                wd = slice(INNER + i * P, INNER + (i + 1) * P)
                for a_, b_ in ((0, 0), (0, 1), (1, 0)):
                    mm = pe.matmul(banks[:, 4 + tb, :], w2[:, w, a_, wd], act2[b_][:, tb % 2, i, :], start=False, stop=last and i == NI - 1 and a_ == 1)
            mm.then_inc(s_down, 1)

        def expert_act(act, q, w, tb, first):
            k = 4 * q + tb
            early = first and tb < 2

            def rounded(i):
                act.wait_ge(s_gh, NI * k + i + 1)
                if i == 0 and not early:
                    act.wait_ge(s_down, k - 1)
                act.activation(act2[0][:, tb % 2, i, :], hid[:, tb % 2, i, :], ACT.Copy).then_inc(s_hh, 1)
            for i in range(NI):
                act.wait_ge(s_up, NI * k + i + 1)
                if i == 0 and not early:
                    act.wait_ge(s_hl, NI * (k - 1))
                act.activation(hid[:, tb % 2, i, :], banks[:, i % 3, :], ACT.Silu, bias=w1[:, w, 2 * INNER + i:2 * INNER + i + 1]).then_inc(s_hid, 1)
                if i >= 2:
                    rounded(i - 2)
            rounded(2)
            rounded(3)

        def expert_dve(dve, q, w, tb, first):
            k = 4 * q + tb
            dve.wait_ge(s_spreadg, k + 1)
            for i in range(NI):
                dve.wait_ge(s_hid, NI * k + i + 1)
                dve.tensor_tensor(hid[:, tb % 2, i, :], hid[:, tb % 2, i, :], banks[:, 3, :], ALU.mult).then_inc(s_gh, 1)

        def expert_pool(pool, q, w, tb, first):
            k = 4 * q + tb
            if not (first and tb < 2):
                pool.wait_ge(s_down, k - 1)
            for i in range(NI):
                pool.wait_ge(s_hh, NI * k + i + 1)
                pool.tensor_tensor(act2[1][:, tb % 2, i, :], hid[:, tb % 2, i, :], act2[0][:, tb % 2, i, :], ALU.subtract).then_inc(s_hl, 1)

        def experts(e, head, tail=None, before=None, split=None):
            def expert(q, w, first, last=False):
                for tb in range(4):
                    if before and tb < 3:
                        before(e, q, tb + 1, first)
                    elif before and not last:
                        before(e, q + 1, 0, False)
                    head(e, q, w, tb, first)
                    if tail and not (first and tb == 0):
                        tail(e, q if tb else q - 1, w if tb else 1 - w, (tb - 1) % 4, first)
                    if split and tb == 1 and not last:
                        split(e, q + 1, 1 - w, first)
            if before:
                before(e, 0, 0, True)
            expert(0, 0, True)
            with e.Fori(0, NE1 // 2 - 1) as m:
                expert(2 * m + 1, 1, False)
                expert(2 * m + 2, 0, False)
            expert(NE1 - 1, 1, False)
            expert(NE1, 0, False, True)
            if tail:
                tail(e, NE1, 0, 3, False)

        def final_act(act):
            for i in range(4):
                act.wait_ge(s_down, 4 * NE1 + i + 1)
                act.activation(yT[:, i, :], banks[:, 4 + i, :], ACT.Copy).then_inc(s_yT, 1)

        def final_pe(pe, i):
            pe.wait_ge(s_yT, i + 1)
            for t in range(4):
                mm = pe.transpose(banks[:, 4 + i, t * P:(t + 1) * P], yT[:, i, t * P:(t + 1) * P], ident)
            mm.then_inc(s_y, 1)

        def final_dve(dve):
            for i in range(4):
                dve.wait_ge(s_y, i + 1)
                xi = x[:, 4 * i:4 * i + 4, :].rearrange("p t d -> p (t d)")
                dve.tensor_tensor(xi, banks[:, 4 + i, :], xi, ALU.add).then_inc(s_xe, 1)

        def x_out(e):
            for i in range(4):
                e.wait_ge(s_xe, i + 1)
                e.dma_start(out[:, 4 * i:4 * i + 4, :], x[:, 4 * i:4 * i + 4, :]).then_inc(s_out, 16)
            e.wait_ge(s_out, 64)

        @block.sync
        def _(sp):
            for i in range(4):
                sp.dma_start(x[:, 4 * i:4 * i + 4, :], a["x"][:, 4 * i:4 * i + 4, :]).then_inc(s_x[i], 16)
            sp.dma_start(cst[:, :], a["cst"]).then_inc(s_const, 16)
            sp.dma_start(wqkv[:, :], a["wqkv"][0]).then_inc(s_wq, 16)
            sp.dma_start(wpr[:, :, :], a["wpr"]).then_inc(s_wp, 16)
            sp.dma_start(bv2[:, :], a["bv2"]).then_inc(s_wp, 16)
            sp.dma_start(pick[:, :, :], a["pick"]).then_inc(s_wp, 16)
            sp.dma_start(mD[:, :, :, :].rearrange("r h s c -> r (h s c)"), a["mD"]).then_inc(s_maskd, 16)
            sp.dma_start(mR[:, :, :], a["mR"]).then_inc(s_maskd, 16)
            for p in range(1, PAIRS):
                sp.wait_ge(s_v, 4 * p)
                sp.wait_ge(s_qk_lo, 16 * p)
                sp.dma_start(wqkv[:, :], a["wqkv"][p]).then_inc(s_wq, 16)
            sp.dma_start(wdn[:, :], a["wdn"]).then_inc(s_fw, 16)
            sp.dma_start(wbase[:, :], a["wbase"]).then_inc(s_fw, 16)
            sp.dma_start(wup[:, :], a["wup"]).then_inc(s_fw, 16)
            sp.dma_start(small[:, :], a["small"]).then_inc(s_fw, 16)
            for t, n in ((wkT, "wkT"), (wvT, "wvT"), (woT, "woT")):
                sp.dma_start(t[:, :], a[n]).then_inc(s_aw, 16)
            sp.dma_start(wk3[:, :], a["wk3"][0]).then_inc(s_wk, 16)
            for t, n in ((wr, "wr"), (wr2, "wr2"), (b2, "b2")):
                sp.dma_start(t[:, :], a[n]).then_inc(s_mw, 16)
            for q in range(2):
                sp.dma_start(w1[:, q, :], a["experts"][q]).then_inc(s_ew[q], 16)
            for g in range(1, GROUPS):
                sp.wait_ge(s_pj, 4 * g)
                sp.dma_start(wk3[:, :], a["wk3"][g]).then_inc(s_wk, 16)
            for q in range(2, 1 + NE1):
                sp.wait_ge(s_ws, 2 * (q - 1))
                sp.wait_ge(s_hid, 4 * NI * (q - 1))
                sp.dma_start(w1[:, q % 2, :], a["experts"][q]).then_inc(s_ew[q % 2], 16)
            x_out(sp)

        @block.gpsimd
        def _(pool):
            pool.memset(zero[:, :], 0.0).then_inc(s_setup, 1)
            pool.wait_ge(s_setup, N_SETUP)

            def padd(e, u, b, j, first):
                h, sbk, t, o = unit(j)
                if t == 0 and h == 0 and not first:
                    e.wait_ge(s_sum, 2 * u + sbk - 1)
                elif t > 0:
                    e.wait_ge(s_padd, NU * u + j - 1)
                e.wait_ge(s_exp, NU * u + j + 1)
                src = zero[:, :] if t == 0 else pacc[:, sbk, h, o:BLK]
                e.tensor_tensor(pacc[:, sbk, h, o:BLK], src, pr[:, j % NP0, 0:BLK - o], ALU.add).then_inc(s_padd, 1)
            no = lambda *_: None
            attention0(pool, {}, {}, no, padd, no, no, no)
            experts(pool, expert_pool)

        @block.scalar
        def _(act):
            ln_act(act, 0)

            def exps(e, u, b, j, first):
                h, sbk, t, o = unit(j)
                e.wait_ge(s_st, NU * u + j + 1)
                if not (first and j < NP0):
                    e.wait_ge(s_pv, NU * u + j - NP0 + 1)
                    e.wait_ge(s_padd, NU * u + j - NP0 + 1)
                e.activation(pr[:, j % NP0, 0:BLK - o], banks[:, j % 3, 0:BLK - o], ACT.Exp, scale=SCALE0).then_inc(s_exp, 1)
            no = lambda *_: None
            act.wait_ge(s_cb, 1)
            act.activation(cb[:, :], banks[0:HEADS, 4, 0:D], ACT.Copy, scale=SCALE0).then_inc(s_cbe, 1)
            attention0(act, shares("act"), ends("act"), act_item, exps, act_tail, no, no)
            ln_act(act, 1)
            linear_act(act)
            ln_act(act, 2)
            setup1_act(act)
            attention1(act, prep1_act, slot1_act, no, no)
            ln_act(act, 3)
            gates_act(act)
            experts(act, expert_act)
            final_act(act)

        @block.vector
        def _(dve):
            dve.memset(ones[:, :], 1.0).then_inc(s_setup, 1)
            dve.memset(kb[DH:KB_ROWS, :, :, :].bitcast(F32).rearrange("p b h s -> p (b h s)"), 1.0).then_inc(s_setup, 1)
            dve.memset(mx2[:, :, :], 0.0).then_inc(s_setup, 1)
            ln_dve(dve, 0, lambda e, n: e.wait_ge(s_x[n // 4], 16) if n % 4 == 0 else None)
            dve.wait_ge(s_const, 16)
            for o, c in ((idb, C_ID), (msb, C_MS), (mtb, C_MT)):
                dve.tensor_copy(o[:, :], cst[:, c:c + P]).then_inc(s_setup, 1)
            dve.tensor_copy(spr[:, :], cst[0:RROWS, C_SPR:C_SPR + P]).then_inc(s_setup, 1)

            dve.wait_ge(s_cb, 2)
            dve.wait_ge(ln[0]["norm"], NT)
            for b in range(BATCH):
                for i in range(2):
                    xs = x[:, b * TB + 4 * i:b * TB + 4 * i + 4, :].rearrange("p t d -> p (t d)")
                    dve.tensor_tensor(xs, banks[:, 5 + i, :], xs, ALU.add).then_inc(s_cbe, 1)
            dve.wait_ge(s_cbe, 5)

            dve.wait_ge(s_maskd, 32)
            no = lambda *_: None
            attention0(dve, shares("dve"), ends("dve"), dve_item, no, dve_tail, dve_acc, no)
            dve.memset(hg[:, :, RSUM:RSUM + 1].rearrange("p n o -> p (n o)"), 0.0)
            ln_dve(dve, 1, lambda e, n: e.wait_ge(s_xacc, 2 * PAIRS) if n == 0 else None)
            linear_dve(dve)
            ln_dve(dve, 2, lambda e, n: e.wait_ge(s_fx, n // 4 + 1) if n % 4 == 0 else None)
            setup1_dve(dve)
            attention1(dve, prep1_dve, no, sums1_dve, out1_dve)
            dve.memset(rT[RH:RH + 1, :], 1.0).then_inc(s_rhe, 1)
            ln_dve(dve, 3, lambda e, n: e.wait_ge(s_x1, 4 * GROUPS) if n == 0 else None)
            gates_dve(dve)
            experts(dve, expert_dve, before=lambda e, q, tb, first: select_dve(e, q, tb, first), split=split_dve)
            final_dve(dve)

        @block.tensor
        def _(pe):
            pe.wait_ge(s_const, 16)
            ln_pe(pe, 0)
            pe.wait_ge(ln[0]["xT"], 4)
            pe.wait_ge(s_setup, N_SETUP)
            pe.wait_ge(s_wp, 48)
            for i in range(TB):
                mm = pe.matmul(banks[0:HEADS, 4, 0:D], bv2[:, :], wpr[:, i, :], start=(i == 0), stop=(i == TB - 1))
            mm.then_inc(s_cb, 1)
            pe.wait_ge(s_cbe, 1)
            for p in range(TB):
                mm = pe.matmul(banks[:, 5 + p // 4, (p % 4) * P:(p % 4 + 1) * P], pick[:, p, :], cb[:, :], start=True, stop=True)
            mm.then_inc(s_cb, 1)

            def rest(e, u, b, j, first):
                for k in ([j - 3, j - 2] if j % 2 and j >= 3 else []) + ([j - 1, j] if j == NU - 1 else []):
                    pe_pv(e, u, b, k, first)
            attention0(pe, shares("pe"), ends("pe"), pe_item, pe_scores, pe_tail, pe_out, rest)
            ln_pe(pe, 1)
            linear_pe(pe)
            ln_pe(pe, 2)
            setup1_pe(pe)
            attention1(pe, prep1_pe, slot1_pe, sums1_pe, out1_pe)
            ln_pe(pe, 3)
            gates_pe(pe)
            bias_pe(pe)
            experts(pe, up_pe, down_pe)
            for i in range(4):
                final_pe(pe, i)


def kernel(**inp):
    import concourse.bacc as bacc
    from concourse.bass_utils import run_bass_kernel_spmd

    f = {k: np.ascontiguousarray(t) for k, t in inp.items()}

    def pairs(w):
        return w.reshape(PAIRS, 2 * DH, D).transpose(0, 2, 1)

    def rows(b):
        return b.reshape(PAIRS, 2 * DH, 1)

    cst, mr, m, pick = constants()
    arrays = {
        "x": f["L0_attn_x"].reshape(NT, P, D).transpose(1, 0, 2),
        "cst": cst,
        "mD": m,
        "mR": mr,
        "wqkv": np.concatenate([pairs(f["L0_attn_Wq"]), pairs(f["L0_attn_Wk"]), pairs(f["L0_attn_Wv"]),
                                rows(f["L0_attn_bq"]), rows(f["L0_attn_bk"])], axis=2),
        "bv2": np.tile(f["L0_attn_bv"].T, (2, 1)),
        "pick": pick,
        "wpr": f["L0_attn_proj"].reshape(TB, P, D).transpose(1, 0, 2),
    }
    ranks = range(NE0)
    zeros = np.zeros((1, D), np.float32)
    arrays |= {
        "wdn": np.concatenate([f["L0_ffn_Wp"]] + [f[f"L0_ffn_Wd{i}"] for i in ranks] + [zeros]).T,
        "wbase": f["L0_ffn_W"].T,
        "wup": np.concatenate([f[f"L0_ffn_Wu{i}"].T for i in ranks] + [zeros]),
        "small": np.broadcast_to(np.concatenate([f["L0_ffn_bp"], f["L0_ffn_sim"].T.reshape(-1), f["L0_ffn_temp"]]),
                                 (P, PROJ + NE0 * PROJ + 1)),
        "wkT": f["L1_attn_W_k"].T,
        "wvT": f["L1_attn_W_v"].T,
        "woT": f["L1_attn_W_o"].T,
        "wk3": np.stack([np.tile(w.T, (1, 3)) for w in f["L1_attn_W_k"].reshape(GROUPS, GH * DK, D)]),
        "wr": np.concatenate([f["L1_ffn_Wr1"], np.resize(f["L1_ffn_br1"], (P, 1))], axis=1),
        "wr2": np.concatenate([f["L1_ffn_Wr2"], f["L1_ffn_br2"][None]]),
        "b2": np.concatenate([f["L1_ffn_bs2"][None], f["L1_ffn_be2"]] * 2),
        "experts": np.stack([np.concatenate([up, down.reshape(NI, P, D).transpose(1, 0, 2).reshape(P, INNER), bias.reshape(NI, P).T],
                                            axis=1)
                             for up, down, bias in zip([f["L1_ffn_Ws1"], *f["L1_ffn_We1"]], [f["L1_ffn_Ws2"], *f["L1_ffn_We2"]],
                                                       [f["L1_ffn_bs1"], *f["L1_ffn_be1"]])]),
    }
    arrays = {k: np.ascontiguousarray(t) for k, t in arrays.items()}
    nc = bacc.Bacc("TRN2", target_bir_lowering=False, num_devices=1)
    a = {k: nc.dram_tensor(f"in_{k}", t.shape, F32, kind="ExternalInput").ap() for k, t in arrays.items()}
    out = nc.dram_tensor("out", (P, NT, D), F32, kind="ExternalOutput").ap()
    build_kernel(nc, a, out, None)
    r = run_bass_kernel_spmd(nc, [{f"in_{k}": t for k, t in arrays.items()}], core_ids=[0])
    y = np.asarray(r.results[0]["out"]).reshape(P, NT, D)
    return np.ascontiguousarray(y.transpose(1, 0, 2)).reshape(BATCH, SEQ, D)
```
